# Optimizing a Trainium2 kernel written in Bass

```python
import numpy as np
import jax
import jax.numpy as jnp

def _softmax(x, axis=-1):
    return jax.nn.softmax(x, axis=axis)

def _gelu(x):
    return jax.nn.gelu(x, approximate=True)

def _silu(x):
    return jax.nn.silu(x)

def _sigmoid(x):
    return jax.nn.sigmoid(x)

def _layernorm(x, axis=-1, eps=1e-05):
    m = jnp.mean(x, axis=axis, keepdims=True)
    v = jnp.var(x, axis=axis, keepdims=True)
    return (x - m) / jnp.sqrt(v + eps)

def _scatter_add(tgt, idx, src, axis=0):
    return tgt.at[idx].add(src)

def _segment_sum(src, seg, n):
    return jax.ops.segment_sum(src, seg, n)
kernel_name = 'mk_audio_tower_d1_tok_aud1d512_r4_4b5a0a'

def setup_inputs(seed: int=0):
    np.random.seed(seed)
    _w = jnp.asarray

    def _rec_inputs():
        import jax
        import jax.numpy as jnp
        _rk = jax.random.key(seed)
        x = 0.000265968 + 1.00011 * jax.random.normal(jax.random.fold_in(_rk, 1), (16, 120000), jnp.float32)
        return x
    x = _rec_inputs()

    def _L0_tok_setup():
        import jax, jax.numpy as jnp
        import numpy as np
        FRAME_LENGTH = 256

        def _mdct_matrix(L2):
            L = L2 // 2
            n = np.arange(L2, dtype=np.float64) + 0.5
            k = np.pi / L * n[:L]
            n2 = n + L / 2
            z = np.sqrt(4.0 / L)
            W = z * np.cos(np.outer(n2, k))
            return jnp.asarray(W, dtype=jnp.float32)

        def _sine_window(L2):
            n = np.arange(L2, dtype=np.float64)
            return jnp.asarray(np.sin(np.pi * (n + 0.5) / L2), dtype=jnp.float32)
        key = jax.random.key(seed)
        x = jax.random.normal(key, (16, 262144), dtype=jnp.float32)
        return {'x': x}
    _L0_tok_all = _L0_tok_setup()
    _L0_tok_in = {k: v for k, v in _L0_tok_all.items() if k in ()}
    del _L0_tok_all

    def _L0_attn_setup():
        import jax, jax.numpy as jnp
        import numpy as np
        B, T, C, NB = (4, 1024, 128, 64)
        key = jax.random.key(seed)
        ks = jax.random.split(key, 6)
        s = 0.02
        return {'x': jax.random.normal(ks[0], (B, T, C), dtype=jnp.float32), 'basis': jax.random.normal(ks[1], (C, 2 * NB), dtype=jnp.float32), 'q_coeffs': jax.random.normal(ks[2], (C, 2 * NB), dtype=jnp.float32) * s, 'k_coeffs': jax.random.normal(ks[3], (C, 2 * NB), dtype=jnp.float32) * s, 'v_coeffs': jax.random.normal(ks[4], (C, 2 * NB), dtype=jnp.float32) * s, 'o_coeffs': jax.random.normal(ks[5], (C, 2 * NB), dtype=jnp.float32) * s, 'decay_logit': jnp.float32(3.0), 'out_scale': jnp.float32(0.1)}
    _L0_attn_all = _L0_attn_setup()
    _L0_attn_in = {k: v for k, v in _L0_attn_all.items() if k in ('basis', 'q_coeffs', 'k_coeffs', 'v_coeffs', 'o_coeffs', 'decay_logit', 'out_scale')}
    del _L0_attn_all

    def _L0_ffn_setup():
        import jax, jax.numpy as jnp
        import numpy as np
        DIM = 128
        HID = 256
        E = 8
        K = 2
        B, S = (4, 512)
        key = jax.random.key(seed)
        ks = jax.random.split(key, 10)
        sd = DIM ** (-0.5)
        sh = HID ** (-0.5)
        return {'x': jax.random.normal(ks[0], (B, S, DIM), dtype=jnp.float32), 'gate_w': jax.random.normal(ks[1], (E, DIM), dtype=jnp.float32) * sd, 'biases': jnp.zeros((E,), dtype=jnp.float32), 'w1': jax.random.normal(ks[2], (E, DIM, HID), dtype=jnp.float32) * sd, 'w3': jax.random.normal(ks[3], (E, DIM, HID), dtype=jnp.float32) * sd, 'w2': jax.random.normal(ks[4], (E, HID, DIM), dtype=jnp.float32) * sh, 'sw1': jax.random.normal(ks[5], (DIM, HID), dtype=jnp.float32) * sd, 'sw3': jax.random.normal(ks[6], (DIM, HID), dtype=jnp.float32) * sd, 'sw2': jax.random.normal(ks[7], (HID, DIM), dtype=jnp.float32) * sh}
    _L0_ffn_all = _L0_ffn_setup()
    _L0_ffn_in = {k: v for k, v in _L0_ffn_all.items() if k in ('gate_w', 'biases', 'w1', 'w3', 'w2', 'sw1', 'sw3', 'sw2')}
    del _L0_ffn_all
    return {'x': x, 'L0_attn_basis': _L0_attn_in['basis'], 'L0_attn_q_coeffs': _L0_attn_in['q_coeffs'], 'L0_attn_k_coeffs': _L0_attn_in['k_coeffs'], 'L0_attn_v_coeffs': _L0_attn_in['v_coeffs'], 'L0_attn_o_coeffs': _L0_attn_in['o_coeffs'], 'L0_attn_decay_logit': _L0_attn_in['decay_logit'], 'L0_attn_out_scale': _L0_attn_in['out_scale'], 'L0_ffn_gate_w': _L0_ffn_in['gate_w'], 'L0_ffn_biases': _L0_ffn_in['biases'], 'L0_ffn_w1': _L0_ffn_in['w1'], 'L0_ffn_w3': _L0_ffn_in['w3'], 'L0_ffn_w2': _L0_ffn_in['w2'], 'L0_ffn_sw1': _L0_ffn_in['sw1'], 'L0_ffn_sw3': _L0_ffn_in['sw3'], 'L0_ffn_sw2': _L0_ffn_in['sw2']}

def reference(x, L0_attn_basis, L0_attn_q_coeffs, L0_attn_k_coeffs, L0_attn_v_coeffs, L0_attn_o_coeffs, L0_attn_decay_logit, L0_attn_out_scale, L0_ffn_gate_w, L0_ffn_biases, L0_ffn_w1, L0_ffn_w3, L0_ffn_w2, L0_ffn_sw1, L0_ffn_sw3, L0_ffn_sw2):
    import jax
    import jax.numpy as jnp

    def _L0_tok_ref(x):
        import jax, jax.numpy as jnp
        import numpy as np
        FRAME_LENGTH = 256

        def _mdct_matrix(L2):
            L = L2 // 2
            n = np.arange(L2, dtype=np.float64) + 0.5
            k = np.pi / L * n[:L]
            n2 = n + L / 2
            z = np.sqrt(4.0 / L)
            W = z * np.cos(np.outer(n2, k))
            return jnp.asarray(W, dtype=jnp.float32)

        def _sine_window(L2):
            n = np.arange(L2, dtype=np.float64)
            return jnp.asarray(np.sin(np.pi * (n + 0.5) / L2), dtype=jnp.float32)
        L2 = FRAME_LENGTH
        hop = L2 // 2
        x = jnp.pad(x, ((0, 0), (0, hop)))
        x = jnp.pad(x, ((0, 0), (L2 // 2, (L2 - 1) // 2)))
        T = x.shape[-1]
        n_frames = (T - L2) // hop + 1
        idx = jnp.arange(n_frames)[:, None] * hop + jnp.arange(L2)[None, :]
        frames = x[:, idx]
        w = _sine_window(L2)
        W = _mdct_matrix(L2)
        return jnp.einsum('bfl,l,lk->bfk', frames, w, W)

    def _L0_attn_ref(x, basis, q_coeffs, k_coeffs, v_coeffs, o_coeffs, decay_logit, out_scale):
        import jax, jax.numpy as jnp
        import numpy as np
        B, T, C, NB = (4, 1024, 128, 64)
        dtype = x.dtype
        q_w = (basis @ q_coeffs.T).astype(dtype)
        k_w = (basis @ k_coeffs.T).astype(dtype)
        v_w = (basis @ v_coeffs.T).astype(dtype)
        o_w = (basis @ o_coeffs.T).astype(dtype)
        queries = x @ q_w
        keys = x @ k_w
        values = x @ v_w
        scores = jnp.einsum('btc,bsc->bts', queries, keys)
        decay = jax.nn.sigmoid(decay_logit)
        pos = jnp.arange(x.shape[1])
        diff = pos[None, :] - pos[:, None]
        expo = jnp.maximum(diff - 1, 0).astype(dtype)
        weights = jnp.where(diff > 0, jnp.power(decay.astype(dtype), expo), jnp.zeros((), dtype))
        scores = scores * weights[None, :, :]
        retrieved = jnp.einsum('bts,bsc->btc', scores, values)
        return retrieved @ o_w.T * out_scale.astype(dtype)

    def _L0_ffn_ref(x, gate_w, biases, w1, w3, w2, sw1, sw3, sw2):
        import jax, jax.numpy as jnp
        import numpy as np
        DIM = 128
        HID = 256
        E = 8
        K = 2
        B, S = (4, 512)
        Bb, Ss, D = x.shape
        xt = x.reshape(Bb * Ss, D)
        shared = jax.nn.silu(xt @ sw1) * (xt @ sw3) @ sw2
        scores = xt @ gate_w.T
        _, idx = jax.lax.top_k(scores + biases, K)
        topv, _ = jax.lax.top_k(scores, K)
        p = jax.nn.sigmoid(topv)
        p = p / jnp.sum(p, axis=-1, keepdims=True)
        h = jax.nn.silu(jnp.einsum('td,edh->eth', xt, w1)) * jnp.einsum('td,edh->eth', xt, w3)
        y = jnp.einsum('eth,ehd->etd', h, w2)
        onehot = jax.nn.one_hot(idx, E, dtype=xt.dtype)
        comb = jnp.einsum('tk,tke->te', p, onehot)
        out = jnp.einsum('te,etd->td', comb, y) + shared
        return out.reshape(Bb, Ss, D)
    h = _L0_tok_ref(x)
    h = h + _L0_attn_ref(_layernorm(h, axis=-1), L0_attn_basis, L0_attn_q_coeffs, L0_attn_k_coeffs, L0_attn_v_coeffs, L0_attn_o_coeffs, L0_attn_decay_logit, L0_attn_out_scale)
    h = h + _L0_ffn_ref(_layernorm(h, axis=-1), L0_ffn_gate_w, L0_ffn_biases, L0_ffn_w1, L0_ffn_w3, L0_ffn_w2, L0_ffn_sw1, L0_ffn_sw3, L0_ffn_sw2)
    return h

_drawn_inputs = setup_inputs


def setup_inputs(seed=0):
    import zlib

    import numpy as np

    out = dict(_drawn_inputs(seed))
    spreads = {'L0_ffn_biases': (0.0, 0.8)}
    factors = {'L0_ffn_gate_w': 8.0,
     'L0_ffn_w1': 8.0,
     'L0_ffn_w3': 8.0,
     'L0_ffn_w2': 8.0,
     'L0_ffn_sw1': 8.0,
     'L0_ffn_sw3': 8.0,
     'L0_ffn_sw2': 8.0}
    for name, (base, spread) in spreads.items():
        noise = np.random.default_rng([zlib.crc32(name.encode()), seed]).standard_normal(out[name].shape)
        drawn = base * np.exp(spread * noise) if base else spread * noise
        out[name] = jnp.asarray(drawn.astype(out[name].dtype))
    for name, factor in factors.items():
        out[name] = (out[name] * factor).astype(out[name].dtype)
    return out
```

```python
from contextlib import ExitStack

import numpy as np

import concourse.bass as bass
from concourse import mybir

F32 = mybir.dt.float32
U32 = mybir.dt.uint32
ALU = mybir.AluOpType
ACT = mybir.ActivationFunctionType
AX = mybir.AxisListType

B = 16
SAMPLES = 120000
C = 128
FRAMES = 939
L = 120
TILES = 8
HT = TILES // 2
HTOK = HT * L
PTOK = TILES * L
REST = FRAMES - (TILES - 1) * L
CHUNKS = PTOK + 1
HID = 256
HC = HID // C
E = 8
BITS = 7
EPS = 1e-5


def positive(n):
    return not isinstance(n, int) or n > 0


def cap(n, top):
    return min(n, top) if isinstance(n, int) else n


def audio_tower(nc, x_t, w_tok, basis_t, qc_t, kc_t, vc_t, oc_t, decay_logit, out_scale, gate_t,
                biases, w1, w3, w2, exp_bits, causal, ident, out):
    with ExitStack() as ctx:
        def sb(name, shape, dt=F32):
            return ctx.enter_context(nc.sbuf_tensor(name, shape, dt))

        def sem(name):
            return ctx.enter_context(nc.semaphore(name))

        w_tok_s = sb("w_tok_s", [C, 2, C])
        coef = sb("coef", [C, 5, C])
        proj_t = sb("proj_t", [C, 4, C])
        wqk = sb("wqk", [C, C])
        wvo = sb("wvo", [C, C])
        gate_s = sb("gate_s", [C, E])
        bias_s = sb("bias_s", [C, E])
        w1_s = sb("w1_s", [C, E + 1, HID])
        w3_s = sb("w3_s", [C, E + 1, HID])
        w2_s = sb("w2_s", [C, E + 1, HC, C])
        ident_s = sb("ident_s", [C, C])
        scal = sb("scal", [C, 2])
        powers = sb("powers", [C, BITS + 1])
        decay_rev = sb("decay_rev", [C, C])
        decay_len = sb("decay_len", [C, 1])
        bits_s = sb("bits_s", [L, BITS, L + 1])
        causal_s = sb("causal_s", [L, L + 1])
        factor = sb("factor", [L, L + 1])
        mask = sb("mask", [L, L + 1])
        half_neg = sb("half_neg", [L, TILES])

        resid = sb("resid", [L, B, TILES * C])
        x_in = [sb(f"x_in{u}", [C, CHUNKS]) for u in range(2)]
        xn = [sb(f"xn{u}", [L, TILES, C]) for u in range(2)]
        xn_dec = [sb(f"xn_dec{u}", [L, TILES, C]) for u in range(2)]
        xn_t = [sb(f"xn_t{u}", [C, PTOK]) for u in range(2)]
        q_t = [sb(f"q_t{u}", [C, PTOK]) for u in range(2)]
        q_dec = [sb(f"q_dec{u}", [C, PTOK]) for u in range(2)]
        prob = [sb(f"prob{u}", [L, PTOK]) for u in range(2)]
        state = [sb(f"state{u}", [C, TILES, C]) for u in range(2)]
        ret_t = sb("ret_t", [C, PTOK])
        xn2 = [sb(f"xn2{u}", [L, TILES, C]) for u in range(2)]
        xn2_t = sb("xn2_t", [C, PTOK])
        stats = sb("stats", [L, TILES, 6])
        mv1 = sb("mv1", [L, TILES, 2])
        mv2 = sb("mv2", [L, TILES, 2])
        ve1 = sb("ve1", [L, TILES])
        ve2 = sb("ve2", [L, TILES])
        rstd1 = sb("rstd1", [L, TILES])
        rstd2 = sb("rstd2", [L, TILES])
        raw = sb("raw", [L, TILES, E])
        biased = sb("biased", [L, TILES, E])
        top_raw = sb("top_raw", [L, TILES, 8])
        top_biased = sb("top_biased", [L, TILES, 8])
        top_idx = sb("top_idx", [L, TILES, 8], U32)
        idx_f = sb("idx_f", [L, TILES, 2])
        sig = sb("sig", [L, TILES, 2])
        sig_sum = sb("sig_sum", [L, TILES])
        sig_rec = sb("sig_rec", [L, TILES])
        iota_e = sb("iota_e", [L, E])
        comb = sb("comb", [L, TILES, E])
        comb1 = sb("comb1", [L, TILES, E])
        gated = sb("gated", [C, HTOK])
        hid = [sb(f"hid{u}", [C, HC, HTOK]) for u in range(2)]

        ps = [ctx.enter_context(nc.psum_tensor(f"bank{i}", [C, 512], F32)) for i in range(8)]
        P_H, P_TR, P_QR, P_G, P_O, P_A1, P_A3, P_S = ps

        w_loaded = sem("w_loaded")
        proj_psum, proj_saved = sem("proj_psum"), sem("proj_saved")
        fold_psum, fold_saved = sem("fold_psum"), sem("fold_saved")
        dsig_ready, pw_step, mask_step, consts_ready = sem("dsig_ready"), sem("pw_step"), sem("mask_step"), sem("consts_ready")
        passed_dve, passed_pool = sem("passed_dve"), sem("passed_pool")
        half_set, iota_set = sem("half_set"), sem("iota_set")
        x_loaded = [sem(f"x_loaded{u}") for u in range(2)]
        h_psum, h_saved = sem("h_psum"), sem("h_saved")
        stat_done, mean_done, ve1_done, rstd1_ready = sem("stat_done"), sem("mean_done"), sem("ve1_done"), sem("rstd1_ready")
        xn_ready, xn_dec_ready = sem("xn_ready"), sem("xn_dec_ready")
        xn_t_psum, xn_t_ready = sem("xn_t_psum"), sem("xn_t_ready")
        q_psum, q_ready, q_dec_ready = sem("q_psum"), sem("q_ready"), sem("q_dec_ready")
        g_psum, state_step = sem("g_psum"), sem("state_step")
        s_psum, prob_ready = sem("s_psum"), sem("prob_ready")
        r_psum, ret_ready = sem("r_psum"), sem("ret_ready")
        o_psum, h2_ready = sem("o_psum"), sem("h2_ready")
        stat2_done, mean2_done, ve2_done, rstd2_ready = sem("stat2_done"), sem("mean2_done"), sem("ve2_done"), sem("rstd2_ready")
        xn2_ready = sem("xn2_ready")
        xn2_t_psum, xn2_t_ready = sem("xn2_t_psum"), sem("xn2_t_ready")
        gate_psum, gate_saved = sem("gate_psum"), sem("gate_saved")
        route_step, sig_ready, comb_step = sem("route_step"), sem("sig_ready"), sem("comb_step")
        a1_psum, a3_psum, gated_ready, hid_ready = sem("a1_psum"), sem("a3_psum"), sem("gated_ready"), sem("hid_ready")
        y_psum, y_added = sem("y_psum"), sem("y_added")
        out_stored = sem("out_stored")

        HALVES = (1, 0)
        NEXP = E + 1
        NW = 15
        block = ctx.enter_context(nc.Block())

        def stages(it, u):
            def stage(lag):
                n = it - lag
                if isinstance(n, int) and not 0 <= n < B:
                    return None
                return n, (u - lag) % 2
            return [stage(lag) for lag in range(4)]

        def steps(eng, step):
            for it in range(4):
                step(it, it // 2, it % 2)
            with eng.Fori(0, (B - 4) // 2) as i:
                for u in range(2):
                    step(i * 2 + (4 + u), i + 2, u)
            for it in range(B, B + 3):
                step(it, it // 2, it % 2)

        @block.sync
        def _(sp):
            for dst, src in ((w_tok_s[:], w_tok), (coef[:, 0, :], basis_t), (coef[:, 1, :], qc_t),
                             (coef[:, 2, :], kc_t), (coef[:, 3, :], vc_t), (coef[:, 4, :], oc_t),
                             (scal[:, 0:1], decay_logit), (scal[:, 1:2], out_scale),
                             (bits_s[:], exp_bits), (causal_s[:], causal), (ident_s[:], ident),
                             (gate_s[:], gate_t), (bias_s[:], biases)):
                sp.dma_start(dst, src).then_inc(w_loaded, 16)

            def step(it, pair, u):
                s1 = stages(it, u)[0]
                if s1:
                    b, _ = s1
                    if positive(2 * b - 2):
                        sp.wait_ge(h_psum, 2 * b - 2)
                    sp.dma_start(x_in[u][:], x_t[:, b, :]).then_inc(x_loaded[u], 16)
            steps(sp, step)

        @block.gpsimd
        def _(pool):
            nc.gpsimd.memset(half_neg[:], -0.5).then_inc(half_set, 1)
            nc.gpsimd.iota(iota_e[:], [[1, E]], base=0, channel_multiplier=0,
                           allow_small_or_imprecise_dtypes=True).then_inc(iota_set, 1)
            pool.wait_ge(half_set, 1)
            pool.wait_ge(consts_ready, 1)

            def step(it, pair, u):
                s1, _, s3, _ = stages(it, u)
                if s1:
                    b, _ = s1
                    pool.wait_ge(mean_done, b + 1)
                    pool.sem_inc(passed_pool, 1)
                    nc.gpsimd.tensor_scalar(ve1[:], mv1[:, :, 1], EPS, None, ALU.add).then_inc(ve1_done, 1)
                    pool.wait_ge(ve1_done, b + 1)
                    nc.gpsimd.tensor_tensor(rstd1[:], ve1[:], half_neg[:], ALU.pow).then_inc(rstd1_ready, 1)
                if s3:
                    b, _ = s3
                    pool.wait_ge(mean2_done, b + 1)
                    pool.sem_inc(passed_pool, 1)
                    nc.gpsimd.tensor_scalar(ve2[:], mv2[:, :, 1], EPS, None, ALU.add).then_inc(ve2_done, 1)
                    pool.wait_ge(ve2_done, b + 1)
                    nc.gpsimd.tensor_tensor(rstd2[:], ve2[:], half_neg[:], ALU.pow).then_inc(rstd2_ready, 1)
                if s1:
                    b, _ = s1
                    pool.wait_ge(xn_ready, b + 1)
                    if positive(2 * b - 2):
                        pool.wait_ge(g_psum, 2 * b - 2)
                    pool.sem_inc(passed_pool, 1)
                    nc.gpsimd.tensor_scalar(xn_dec[u][:], xn[u][:], mask[:, 0:1], None, ALU.mult)\
                        .then_inc(xn_dec_ready, 1)
            steps(pool, step)

        @block.scalar
        def _(act):
            for dst, src in ((w1_s[:], w1), (w3_s[:], w3)):
                act.dma_start(dst, src).then_inc(w_loaded, 16)
            act.dma_start(w2_s[:], w2).then_inc(w_loaded, 16)
            act.wait_ge(w_loaded, 16 * 16)
            nc.scalar.activation(powers[:, 0:1], scal[:, 0:1], ACT.Sigmoid).then_inc(dsig_ready, 1)
            act.wait_ge(proj_psum, 1)
            nc.scalar.copy(proj_t[:], P_H[:]).then_inc(proj_saved, 1)
            act.wait_ge(fold_psum, 1)
            nc.scalar.copy(wqk[:], P_TR[:, 0:C]).then_inc(fold_saved, 1)
            nc.scalar.activation(wvo[:], P_TR[:, C:2 * C], ACT.Copy, scale=scal[:, 1:2]).then_inc(fold_saved, 1)

            def step(it, pair, u):
                s1, s2, s3, s4 = stages(it, u)

                def save_h(b, o):
                    act.wait_ge(h_psum, 2 * b + o + 1)
                    nc.scalar.copy(resid[:, b, o * 512:(o + 1) * 512], P_H[0:L, :]).then_inc(h_saved, 1)

                def save_xn_t(b, v, o):
                    hf = HALVES[o]
                    act.wait_ge(xn_t_psum, 2 * b + o + 1)
                    if positive(2 * b - 2):
                        act.wait_ge(s_psum, 2 * b - 2)
                    nc.scalar.copy(xn_t[v][:, hf * HTOK:(hf + 1) * HTOK], P_TR[:, 0:HTOK]).then_inc(xn_t_ready, 1)

                def save_ret(b, o):
                    hf = HALVES[o]
                    act.wait_ge(r_psum, 2 * b + o + 1)
                    if positive(2 * b):
                        act.wait_ge(o_psum, 2 * b)
                    nc.scalar.copy(ret_t[:, hf * HTOK:(hf + 1) * HTOK], P_QR[:, 0:HTOK]).then_inc(ret_ready, 1)

                def save_q(b, v, o):
                    hf = HALVES[o]
                    act.wait_ge(q_psum, 2 * b + o + 1)
                    if positive(2 * b - 2):
                        act.wait_ge(q_dec_ready, 2 * b - 2)
                    nc.scalar.copy(q_t[v][:, hf * HTOK:(hf + 1) * HTOK], P_QR[:, 0:HTOK]).then_inc(q_ready, 1)

                if s1:
                    save_h(s1[0], 0)
                if s2:
                    save_xn_t(*s2, 0)
                if s3:
                    save_ret(s3[0], 0)
                if s1:
                    save_h(s1[0], 1)
                if s2:
                    save_xn_t(*s2, 1)
                if s3:
                    save_ret(s3[0], 1)
                if s2:
                    save_q(*s2, 0)
                    save_q(*s2, 1)
                if s4:
                    b, z = s4
                    for o in range(2):
                        hf = HALVES[o]
                        act.wait_ge(xn2_t_psum, 2 * b + o + 1)
                        if positive(b):
                            act.wait_ge(y_psum, 2 * NEXP * b)
                        nc.scalar.copy(xn2_t[:, hf * HTOK:(hf + 1) * HTOK], P_TR[:, 0:HTOK]).then_inc(xn2_t_ready, 1)
                    act.wait_ge(route_step, 6 * b + 2)
                    nc.scalar.activation(sig[:], top_raw[:, :, 0:2], ACT.Sigmoid).then_inc(sig_ready, 1)
                    for n in range(2 * HC * NEXP):
                        act.wait_ge(a1_psum, 2 * HC * NEXP * b + n + 1)
                        if positive(2 * HC * NEXP * b + n):
                            act.wait_ge(hid_ready, 2 * HC * NEXP * b + n)
                        nc.scalar.activation(gated[:], P_A1[:, 0:HTOK], ACT.Silu).then_inc(gated_ready, 1)
                    act.wait_ge(y_added, 2 * NEXP * (b + 1))
                    act.dma_start(out[b, 0:(TILES - 1) * L, :].rearrange("(j p) d -> p j d", p=L),
                                  resid[:, b, 0:(TILES - 1) * C].rearrange("p (j d) -> p j d", d=C)).then_inc(out_stored, 16)
                    act.dma_start(out[b, (TILES - 1) * L:FRAMES, :],
                                  resid[0:REST, b, (TILES - 1) * C:TILES * C]).then_inc(out_stored, 16)
            steps(act, step)
            act.wait_ge(out_stored, 32 * B)

        @block.vector
        def _(dve):
            dve.wait_ge(dsig_ready, 1)
            nstep = 0
            for n in range(BITS - 1):
                nc.vector.tensor_tensor(powers[:, n + 1:n + 2], powers[:, n:n + 1], powers[:, n:n + 1], ALU.mult).then_inc(pw_step, 1)
                nstep += 1
                dve.wait_ge(pw_step, nstep)
            nc.vector.memset(decay_rev[:, C - 1:C], 1.0).then_inc(pw_step, 1)
            nstep += 1
            for n in range(BITS):
                dve.wait_ge(pw_step, nstep)
                w = 2 ** n
                nc.vector.tensor_scalar(decay_rev[:, C - 2 * w:C - w], decay_rev[:, C - w:C], powers[:, n:n + 1], None, ALU.mult).then_inc(pw_step, 1)
                nstep += 1
            dve.wait_ge(pw_step, nstep)
            nc.vector.tensor_copy(decay_len[:], decay_rev[:, C - 1 - L:C - L]).then_inc(pw_step, 1)
            nc.vector.tensor_copy(mask[:], causal_s[:]).then_inc(mask_step, 1)
            m = 1
            for n in range(BITS):
                dve.wait_ge(mask_step, m)
                nc.vector.tensor_scalar(factor[:], bits_s[:, n, :], -1.0, 1.0, ALU.mult, ALU.add).then_inc(mask_step, 1)
                dve.wait_ge(mask_step, m + 1)
                nc.vector.scalar_tensor_tensor(out=factor[:], in0=bits_s[:, n, :], scalar=powers[0:L, n:n + 1],
                                               in1=factor[:], op0=ALU.mult, op1=ALU.max).then_inc(mask_step, 1)
                dve.wait_ge(mask_step, m + 2)
                last = nc.vector.tensor_tensor(mask[:], mask[:], factor[:], ALU.mult)
                last.then_inc(mask_step, 1)
                m += 3
            dve.wait_ge(mask_step, m)
            dve.wait_ge(pw_step, nstep + 1)
            nc.vector.tensor_scalar(factor[:, 0:1], mask[:, 0:1], 1.0, None, ALU.mult).then_inc(consts_ready, 1)
            dve.wait_ge(iota_set, 1)
            dve.wait_ge(half_set, 1)

            def means(b, src, done, aggregated, mv, count):
                dve.sem_inc(passed_dve, 1)
                for t in range(TILES):
                    last = nc.vector.bn_stats(stats[:, t, :], src[:, t * C:(t + 1) * C])
                last.then_inc(done, 1)
                dve.wait_ge(done, count + 1)
                dve.sem_inc(passed_dve, 1)
                for t in range(TILES):
                    last = nc.vector.bn_aggr(mv[:, t, :], stats[:, t, :])
                last.then_inc(aggregated, 1)

            def step(it, pair, u):
                s1, s2, s3, s4 = stages(it, u)
                if s1:
                    b, _ = s1
                    dve.wait_ge(h_saved, 2 * b + 2)
                    if positive(b):
                        dve.wait_ge(rstd1_ready, b)
                    means(b, resid[:, b, :], stat_done, mean_done, mv1, b)
                for o in range(2):
                    hf = HALVES[o]
                    if s2:
                        b, v = s2
                        cols = slice(hf * HTOK, (hf + 1) * HTOK)
                        dve.wait_ge(q_ready, 2 * b + o + 1)
                        if positive(2 * b - 2):
                            dve.wait_ge(r_psum, 2 * b - 2)
                        nc.vector.tensor_tensor(q_dec[v][:, cols].rearrange("p (j t) -> p j t", t=L),
                                                q_t[v][:, cols].rearrange("p (j t) -> p j t", t=L),
                                                decay_rev[:, C - L:C].unsqueeze(1).to_broadcast([C, HT, L]),
                                                ALU.mult).then_inc(q_dec_ready, 1)
                    if s3:
                        b, w = s3
                        dve.wait_ge(o_psum, 2 * b + o + 1)
                        part = resid[:, b, hf * 512:(hf + 1) * 512]
                        nc.vector.tensor_tensor(part, P_O[0:L, :], part, ALU.add).then_inc(h2_ready, 1)
                if s3:
                    b, w = s3
                    dve.wait_ge(h2_ready, 2 * b + 2)
                    means(b, resid[:, b, :], stat2_done, mean2_done, mv2, b)
                if s2:
                    b, v = s2
                    if positive(2 * b - 2):
                        dve.wait_ge(r_psum, 2 * b - 2)
                    for o in range(2):
                        hf = HALVES[o]
                        dve.wait_ge(g_psum, 2 * b + o + 1)
                        for n, c in enumerate((7, 6, 5, 4) if hf else (3, 2, 1)):
                            part = P_G[:, n * C:(n + 1) * C]
                            if c == TILES - 1:
                                nc.vector.tensor_copy(state[v][:, c - 1, :], part).then_inc(state_step, 1)
                            else:
                                dve.wait_ge(state_step, 7 * b + (7 - c))
                                nc.vector.scalar_tensor_tensor(out=state[v][:, c - 1, :], in0=state[v][:, c, :],
                                                               scalar=decay_len[:, 0:1], in1=part,
                                                               op0=ALU.mult, op1=ALU.add).then_inc(state_step, 1)
                        dve.wait_ge(s_psum, 2 * b + o + 1)
                        cols = slice(hf * HTOK, (hf + 1) * HTOK)
                        nc.vector.tensor_tensor(prob[v][:, cols].rearrange("p (j t) -> p j t", t=L),
                                                P_S[0:L, 0:HTOK].rearrange("p (j t) -> p j t", t=L),
                                                mask[:, 1:L + 1].unsqueeze(1).to_broadcast([L, HT, L]),
                                                ALU.mult).then_inc(prob_ready, 1)
                if s1:
                    b, _ = s1
                    dve.wait_ge(rstd1_ready, b + 1)
                    if positive(2 * b - 2):
                        dve.wait_ge(r_psum, 2 * b - 2)
                    if positive(b - 1):
                        dve.wait_ge(xn_dec_ready, b - 1)
                    for t in range(TILES):
                        last = nc.vector.tensor_scalar(xn[u][:, t, :], resid[:, b, t * C:(t + 1) * C],
                                                       mv1[:, t, 0:1], rstd1[:, t:t + 1], ALU.subtract, ALU.mult)
                    last.then_inc(xn_ready, 1)
                if s3:
                    b, w = s3
                    dve.wait_ge(rstd2_ready, b + 1)
                    if positive(2 * b - 2):
                        dve.wait_ge(xn2_t_psum, 2 * b - 2)
                    for t in range(TILES):
                        last = nc.vector.tensor_scalar(xn2[w][:, t, :], resid[:, b, t * C:(t + 1) * C],
                                                       mv2[:, t, 0:1], rstd2[:, t:t + 1], ALU.subtract, ALU.mult)
                    last.then_inc(xn2_ready, 1)
                if s4:
                    b, z = s4
                    dve.wait_ge(gate_psum, b + 1)
                    if positive(b):
                        dve.wait_ge(sig_ready, b)
                    nc.vector.tensor_copy(raw[:].rearrange("p j e -> p (j e)"), P_O[0:L, 0:TILES * E]).then_inc(route_step, 1)
                    nc.vector.tensor_tensor(biased[:], P_O[0:L, 0:TILES * E].rearrange("p (j e) -> p j e", e=E),
                                            bias_s[0:L, :].unsqueeze(1).to_broadcast([L, TILES, E]), ALU.add).then_inc(gate_saved, 1)
                    dve.wait_ge(route_step, 6 * b + 1)
                    dve.wait_ge(gate_saved, b + 1)
                    dve.sem_inc(passed_dve, 1)
                    for t in range(TILES):
                        nc.vector.max(top_biased[:, t, :], biased[:, t, :])
                        last = nc.vector.max(top_raw[:, t, :], raw[:, t, :])
                    last.then_inc(route_step, 1)
                    dve.wait_ge(route_step, 6 * b + 2)
                    dve.sem_inc(passed_dve, 1)
                    for t in range(TILES):
                        last = nc.vector.max_index(top_idx[:, t, :], top_biased[:, t, :], biased[:, t, :])
                    last.then_inc(route_step, 1)
                    dve.wait_ge(route_step, 6 * b + 3)
                    nc.vector.tensor_copy(idx_f[:], top_idx[:, :, 0:2])
                    dve.wait_ge(sig_ready, b + 1)
                    nc.vector.tensor_tensor(sig_sum[:], sig[:, :, 0], sig[:, :, 1], ALU.add).then_inc(route_step, 1)
                    dve.wait_ge(route_step, 6 * b + 4)
                    nc.vector.reciprocal(sig_rec[:], sig_sum[:])
                    for k, dst in enumerate((comb, comb1)):
                        last = nc.vector.tensor_tensor(dst[:], iota_e[:].unsqueeze(1).to_broadcast([L, TILES, E]),
                                                       idx_f[:, :, k].unsqueeze(2).to_broadcast([L, TILES, E]), ALU.is_equal)
                    last.then_inc(route_step, 1)
                    dve.wait_ge(route_step, 6 * b + 5)
                    for k, dst in enumerate((comb, comb1)):
                        last = nc.vector.tensor_tensor(dst[:], dst[:], sig[:, :, k].unsqueeze(2).to_broadcast([L, TILES, E]), ALU.mult)
                    last.then_inc(route_step, 1)
                    dve.wait_ge(route_step, 6 * b + 6)
                    nc.vector.tensor_tensor(comb1[:], comb[:], comb1[:], ALU.add).then_inc(comb_step, 1)
                    dve.wait_ge(comb_step, 2 * b + 1)
                    nc.vector.tensor_tensor(comb[:], comb1[:], sig_rec[:].unsqueeze(2).to_broadcast([L, TILES, E]), ALU.mult).then_inc(comb_step, 1)
                    dve.wait_ge(comb_step, 2 * b + 2)
                    n = 0
                    for e in range(NEXP):
                        for o in range(2):
                            hf = HALVES[o]
                            for hc in range(HC):
                                g = 2 * HC * NEXP * b + n
                                dve.wait_ge(gated_ready, g + 1)
                                dve.wait_ge(a3_psum, g + 1)
                                if e or True:
                                    w = 2 * NEXP * b + 2 * e + o - 1
                                    if positive(w):
                                        dve.wait_ge(y_psum, w)
                                nc.vector.tensor_tensor(hid[o][:, hc, :], gated[:], P_A3[:, 0:HTOK], ALU.mult).then_inc(hid_ready, 1)
                                n += 1
                            dve.wait_ge(y_psum, 2 * NEXP * b + 2 * e + o + 1)
                            if positive(2 * NEXP * b + 2 * e + o - 1):
                                dve.wait_ge(y_added, 2 * NEXP * b + 2 * e + o - 1)
                            for j in range(HT):
                                t = HT * hf + j
                                part = resid[:, b, t * C:(t + 1) * C]
                                if e < E:
                                    last = nc.vector.scalar_tensor_tensor(out=part, in0=P_O[0:L, j * C:(j + 1) * C], scalar=comb[:, t, e:e + 1],
                                                                          in1=part, op0=ALU.mult, op1=ALU.add)
                                else:
                                    last = nc.vector.tensor_tensor(part, P_O[0:L, j * C:(j + 1) * C], part, ALU.add)
                            last.then_inc(y_added, 1)
            steps(dve, step)

        @block.tensor
        def _(pe):
            pe.wait_ge(w_loaded, 16 * 16)
            for n in range(4):
                last = nc.tensor.matmul(P_H[:, n * C:(n + 1) * C], coef[:, n + 1, :], coef[:, 0, :], start=True, stop=True)
            last.then_inc(proj_psum, 1)
            pe.wait_ge(proj_saved, 1)
            nc.tensor.matmul(P_TR[:, 0:C], proj_t[:, 0, :], proj_t[:, 1, :], start=True, stop=True)
            nc.tensor.matmul(P_TR[:, C:2 * C], proj_t[:, 2, :], proj_t[:, 3, :], start=True, stop=True).then_inc(fold_psum, 1)
            pe.wait_ge(fold_saved, 2)

            def step(it, pair, u):
                s1, s2, s3, s4 = stages(it, u)

                def tokens(b, o):
                    if o == 0:
                        pe.wait_ge(x_loaded[u], 16 * pair + 16)
                    if positive(2 * b + o):
                        pe.wait_ge(h_saved, 2 * b + o)
                    for j in range(HT):
                        m = (HT * o + j) * L
                        nc.tensor.matmul(P_H[0:L, j * C:(j + 1) * C], x_in[u][:, m:m + L], w_tok_s[:, 0, :], start=True, stop=False)
                        last = nc.tensor.matmul(P_H[0:L, j * C:(j + 1) * C], x_in[u][:, m + 1:m + 1 + L], w_tok_s[:, 1, :], start=False, stop=True)
                    last.then_inc(h_psum, 1)

                def turn(b, v, o):
                    if o == 0:
                        pe.wait_ge(xn_ready, b + 1)
                    if positive(2 * b + o):
                        pe.wait_ge(xn_t_ready, 2 * b + o)
                    if positive(2 * b - 4):
                        pe.wait_ge(xn2_t_ready, 2 * b - 4)
                    for j in range(HT):
                        last = nc.tensor.transpose(P_TR[:, j * L:(j + 1) * L], xn[v][:, HT * HALVES[o] + j, :], ident_s[0:L, 0:L])
                    last.then_inc(xn_t_psum, 1)

                def retrieve(b, w, o):
                    if o == 0:
                        pe.wait_ge(prob_ready, 2 * b + 2)
                        pe.wait_ge(state_step, 7 * b + 7)
                        pe.wait_ge(q_dec_ready, 2 * b + 2)
                        pe.wait_ge(q_ready, 2 * b + 2)
                    if positive(2 * b + o):
                        pe.wait_ge(ret_ready, 2 * b + o)
                    for j in range(HT):
                        c = HT * HALVES[o] + j
                        tok = slice(c * L, (c + 1) * L)
                        dst = P_QR[:, j * L:(j + 1) * L]
                        last = nc.tensor.matmul(dst, xn[w][:, c, :], prob[w][:, tok], start=True, stop=(c == TILES - 1))
                        if c < TILES - 1:
                            last = nc.tensor.matmul(dst, state[w][:, c, :], q_dec[w][:, tok], start=False, stop=True)
                    last.then_inc(r_psum, 1)

                def queries(b, v, o):
                    pe.wait_ge(xn_t_ready, 2 * b + o + 1)
                    if positive(2 * b + o):
                        pe.wait_ge(q_ready, 2 * b + o)
                    if positive(2 * b):
                        pe.wait_ge(ret_ready, 2 * b)
                    cols = slice(HALVES[o] * HTOK, (HALVES[o] + 1) * HTOK)
                    nc.tensor.matmul(P_QR[:, 0:HTOK], wqk[:], xn_t[v][:, cols], start=True, stop=True).then_inc(q_psum, 1)

                def project(b, o):
                    pe.wait_ge(ret_ready, 2 * b + o + 1)
                    if positive(2 * b + o):
                        pe.wait_ge(h2_ready, 2 * b + o)
                    if positive(b - 1):
                        pe.wait_ge(y_added, 2 * NEXP * (b - 1))
                    for j in range(HT):
                        c = HT * HALVES[o] + j
                        last = nc.tensor.matmul(P_O[0:L, j * C:(j + 1) * C], ret_t[:, c * L:(c + 1) * L], wvo[:], start=True, stop=True)
                    last.then_inc(o_psum, 1)

                def keys(b, v, o):
                    if o == 0:
                        pe.wait_ge(xn_dec_ready, b + 1)
                    if positive(7 * b + 4 * o):
                        pe.wait_ge(state_step, 7 * b + 4 * o)
                    for n, c in enumerate((3, 2, 1) if o else (7, 6, 5, 4)):
                        last = nc.tensor.matmul(P_G[:, n * C:(n + 1) * C], xn_dec[v][:, c, :], xn[v][:, c, :], start=True, stop=True)
                    last.then_inc(g_psum, 1)

                def scores(b, v, o):
                    pe.wait_ge(q_ready, 2 * b + o + 1)
                    if positive(2 * b + o):
                        pe.wait_ge(prob_ready, 2 * b + o)
                    for j in range(HT):
                        c = HT * HALVES[o] + j
                        tok = slice(c * L, (c + 1) * L)
                        last = nc.tensor.matmul(P_S[0:L, j * L:(j + 1) * L], xn_t[v][:, tok], q_t[v][:, tok], start=True, stop=True)
                    last.then_inc(s_psum, 1)

                if s1:
                    tokens(s1[0], 0)
                if s2:
                    turn(*s2, 0)
                if s3:
                    retrieve(*s3, 0)
                if s1:
                    tokens(s1[0], 1)
                if s2:
                    turn(*s2, 1)
                if s3:
                    retrieve(*s3, 1)
                if s2:
                    queries(*s2, 0)
                if s3:
                    project(s3[0], 0)
                if s2:
                    queries(*s2, 1)
                if s3:
                    project(s3[0], 1)
                if s2:
                    keys(*s2, 0)
                    scores(*s2, 0)
                    keys(*s2, 1)
                    scores(*s2, 1)
                if s4:
                    b, z = s4
                    for o in range(2):
                        if o == 0:
                            pe.wait_ge(xn2_ready, b + 1)
                        if positive(2 * b + o):
                            pe.wait_ge(xn2_t_ready, 2 * b + o)
                        pe.wait_ge(xn_t_ready, cap(2 * b + 6, 2 * B))
                        for j in range(HT):
                            last = nc.tensor.transpose(P_TR[:, j * L:(j + 1) * L], xn2[z][:, HT * HALVES[o] + j, :], ident_s[0:L, 0:L])
                        last.then_inc(xn2_t_psum, 1)
                    pe.wait_ge(xn2_t_ready, 2 * b + 2)
                    pe.wait_ge(h2_ready, cap(2 * b + 4, 2 * B))
                    for c in range(TILES):
                        last = nc.tensor.matmul(P_O[0:L, c * E:(c + 1) * E], xn2_t[:, c * L:(c + 1) * L], gate_s[:], start=True, stop=True)
                    last.then_inc(gate_psum, 1)
                    n = 0
                    for e in range(NEXP):
                        for o in range(2):
                            cols = slice(HALVES[o] * HTOK, (HALVES[o] + 1) * HTOK)
                            for hc in range(HC):
                                g = 2 * HC * NEXP * b + n
                                if positive(g):
                                    pe.wait_ge(gated_ready, g)
                                nc.tensor.matmul(P_A1[:, 0:HTOK], w1_s[:, e, hc * C:(hc + 1) * C], xn2_t[:, cols], start=True, stop=True).then_inc(a1_psum, 1)
                                if positive(g):
                                    pe.wait_ge(hid_ready, g)
                                nc.tensor.matmul(P_A3[:, 0:HTOK], w3_s[:, e, hc * C:(hc + 1) * C], xn2_t[:, cols], start=True, stop=True).then_inc(a3_psum, 1)
                                n += 1
                            pe.wait_ge(hid_ready, 2 * HC * NEXP * b + n)
                            if positive(2 * NEXP * b + 2 * e + o):
                                pe.wait_ge(y_added, 2 * NEXP * b + 2 * e + o)
                            pe.wait_ge(gate_saved, b + 1)
                            for j in range(HT):
                                for hc in range(HC):
                                    last = nc.tensor.matmul(P_O[0:L, j * C:(j + 1) * C], hid[o][:, hc, j * L:(j + 1) * L], w2_s[:, e, hc, :],
                                                            start=(hc == 0), stop=(hc == HC - 1))
                            last.then_inc(y_psum, 1)
            steps(pe, step)


def constants():
    n = np.arange(2 * C, dtype=np.float64) + 0.5
    cosine = np.float32(np.sqrt(4.0 / C) * np.cos(np.outer(n + C / 2, np.pi / C * n[:C]))).astype(np.float64)
    window = np.float32(np.sin(np.pi * n / (2 * C))).astype(np.float64)
    w_tok = (window[:, None] * cosine).astype(np.float32).reshape(2, C, C).transpose(1, 0, 2)
    s, t = np.arange(L)[:, None], np.arange(-1, L)[None, :]
    expo = np.maximum(s - t - 1, 0)
    bits = (expo[:, None, :] >> np.arange(BITS)[None, :, None] & 1).astype(np.float32)
    return {"w_tok": np.ascontiguousarray(w_tok), "exp_bits": bits,
            "causal": (s > t).astype(np.float32), "ident": np.eye(C, dtype=np.float32)}


def kernel(x, L0_attn_basis, L0_attn_q_coeffs, L0_attn_k_coeffs, L0_attn_v_coeffs, L0_attn_o_coeffs,
           L0_attn_decay_logit, L0_attn_out_scale, L0_ffn_gate_w, L0_ffn_biases, L0_ffn_w1, L0_ffn_w3,
           L0_ffn_w2, L0_ffn_sw1, L0_ffn_sw3, L0_ffn_sw2):
    import concourse.bacc as bacc
    from concourse.bass_utils import run_bass_kernel_spmd

    f = np.float32
    padded = np.zeros((B, CHUNKS * C), f)
    padded[:, C:C + SAMPLES] = x
    t = lambda a: np.ascontiguousarray(np.asarray(a).T)
    arrays = constants() | {
        "x_t": np.ascontiguousarray(padded.reshape(B, CHUNKS, C).transpose(2, 0, 1)),
        "basis_t": t(L0_attn_basis), "qc_t": t(L0_attn_q_coeffs), "kc_t": t(L0_attn_k_coeffs),
        "vc_t": t(L0_attn_v_coeffs), "oc_t": t(L0_attn_o_coeffs),
        "decay_logit": np.broadcast_to(np.asarray(L0_attn_decay_logit).reshape(1, 1), (C, 1)).copy(),
        "out_scale": np.broadcast_to(np.asarray(L0_attn_out_scale).reshape(1, 1), (C, 1)).copy(),
        "gate_t": t(L0_ffn_gate_w),
        "biases": np.broadcast_to(np.asarray(L0_ffn_biases)[None, :], (C, E)).copy(),
        "w1": np.ascontiguousarray(np.concatenate([L0_ffn_w1, np.asarray(L0_ffn_sw1)[None]]).transpose(1, 0, 2)),
        "w3": np.ascontiguousarray(np.concatenate([L0_ffn_w3, np.asarray(L0_ffn_sw3)[None]]).transpose(1, 0, 2)),
        "w2": np.ascontiguousarray(np.concatenate([L0_ffn_w2, np.asarray(L0_ffn_sw2)[None]])
                                   .reshape(E + 1, HC, C, C).transpose(2, 0, 1, 3)),
    }
    names = ["x_t", "w_tok", "basis_t", "qc_t", "kc_t", "vc_t", "oc_t", "decay_logit", "out_scale", "gate_t",
             "biases", "w1", "w3", "w2", "exp_bits", "causal", "ident"]
    nc = bacc.Bacc("TRN2", target_bir_lowering=False, num_devices=1)
    args = [nc.dram_tensor(n, arrays[n].shape, mybir.dt.from_np(arrays[n].dtype), kind="ExternalInput").ap() for n in names]
    out = nc.dram_tensor("out", (B, FRAMES, C), F32, kind="ExternalOutput").ap()
    audio_tower(nc, *args, out)
    r = run_bass_kernel_spmd(nc, [arrays], core_ids=[0])
    return r.results[0]["out"]
```

```python
from contextlib import ExitStack

import numpy as np

import concourse.bass as bass
from concourse import mybir

F32 = mybir.dt.float32
BF16 = mybir.dt.bfloat16
I32 = mybir.dt.int32
U32 = mybir.dt.uint32
ALU = mybir.AluOpType
ACT = mybir.ActivationFunctionType
AX = mybir.AxisListType

B = 16
SAMPLES = 120000
C = 128
FRAMES = 939
L = 120
TILES = 8
HT = TILES // 2
HTOK = HT * L
PTOK = TILES * L
REST = FRAMES - (TILES - 1) * L
CHUNKS = PTOK + 1
HID = 256
HC = HID // C
E = 8
BITS = 7
EPS = 1e-5
TOP = 2
P = 128
ROW = C + 4
CAP = B * PTOK + P
SLOTS = (TOP * B * FRAMES + E * (P - 1)) // P
SPARE = SLOTS - -(-TOP * B * FRAMES // P)
ROWS = E * CAP + SPARE * P
RESULTS = TOP * B * PTOK
NOWHERE = 1 << 20


def positive(n):
    return not isinstance(n, int) or n > 0


def cap(n, top):
    return min(n, top) if isinstance(n, int) else n


def audio_tower(nc, x_t, w_tok, basis_t, qc_t, kc_t, vc_t, oc_t, decay_logit, out_scale, gate_t,
                biases, w13, w2, sw1, sw3, sw2, exp_bits, causal, ident, before, pad_idx, pad_dst,
                region, fill_base, tile_no, routed, results, out):
    with ExitStack() as ctx:
        def sb(name, shape, dt=F32):
            return ctx.enter_context(nc.sbuf_tensor(name, shape, dt))

        def sem(name):
            return ctx.enter_context(nc.semaphore(name))

        w_tok_s = sb("w_tok_s", [C, 2, C])
        wqk = sb("wqk", [C, C])
        wvo = sb("wvo", [C, C])
        gate_s = sb("gate_s", [C, E])
        bias_s = sb("bias_s", [C, E])
        w13_s = sb("w13_s", [C, E * 2 * HID])
        w2_s = sb("w2_s", [C, E * HC * C])
        sw1_s = sb("sw1_s", [C, HID])
        sw3_s = sb("sw3_s", [C, HID])
        sw2_s = sb("sw2_s", [C, HC, C])
        ident_s = sb("ident_s", [C, C])
        scal = sb("scal", [C, 2])
        powers = sb("powers", [C, BITS + 1])
        decay_rev = sb("decay_rev", [C, C])
        decay_len = sb("decay_len", [C, 1])
        causal_s = sb("causal_s", [L, L + 1])
        factor = sb("factor", [L, L + 1])
        mask = sb("mask", [L, L + 1])
        half_neg = sb("half_neg", [L, TILES])
        before_f = sb("before_f", [L, L])
        before_s = sb("before_s", [L, L], BF16)
        ones_s = sb("ones_s", [L, P], BF16)
        pad_idx_s = sb("pad_idx_s", [L, TILES * TOP])
        pad_dst_s = sb("pad_dst_s", [L, TILES * TOP])
        region_s = sb("region_s", [L, E])
        fill_base_s = sb("fill_base_s", [P, E])
        tile_no_s = sb("tile_no_s", [1, 2, SLOTS])

        resid = sb("resid", [L, B, TILES * C])
        x_in = [sb(f"x_in{u}", [C, CHUNKS]) for u in range(2)]
        xn = [sb(f"xn{u}", [L, TILES, C]) for u in range(2)]
        xn_dec = [sb(f"xn_dec{u}", [L, TILES, C]) for u in range(2)]
        xn_t = [sb(f"xn_t{u}", [C, PTOK]) for u in range(2)]
        q_t = [sb(f"q_t{u}", [C, PTOK]) for u in range(2)]
        q_dec = [sb(f"q_dec{u}", [C, PTOK]) for u in range(2)]
        prob = [sb(f"prob{u}", [L, PTOK]) for u in range(2)]
        state = [sb(f"state{u}", [C, TILES, C]) for u in range(2)]
        ret_t = sb("ret_t", [C, PTOK])
        xn2 = [sb(f"xn2{u}", [L, TILES, C]) for u in range(2)]
        xn2_t = sb("xn2_t", [C, PTOK])
        stats = sb("stats", [L, TILES, 6])
        mv1 = sb("mv1", [L, TILES, 2])
        mv2 = sb("mv2", [L, TILES, 2])
        ve1 = sb("ve1", [L, TILES])
        ve2 = sb("ve2", [L, TILES])
        rstd1 = sb("rstd1", [L, TILES])
        rstd2 = sb("rstd2", [L, TILES])
        raw = sb("raw", [L, TILES, E])
        biased = sb("biased", [L, TILES, E])
        top_raw = sb("top_raw", [L, TILES, 8])
        top_biased = sb("top_biased", [L, TILES, 8])
        top_idx = sb("top_idx", [L, TILES, 8], U32)
        idx_f = sb("idx_f", [L, TILES * TOP])
        iota_e = sb("iota_e", [L, E])
        chosen = sb("chosen", [L, TILES, TOP, E], BF16)
        assigned = sb("assigned", [L, TILES, E], BF16)
        assigned_sum = sb("assigned_sum", [L, E])
        taken = sb("taken", [L, E], BF16)
        place = sb("place", [L, TILES, E])
        chosen_place = sb("chosen_place", [L, TILES * TOP, E])
        place_sum = sb("place_sum", [L, TILES * TOP])
        dst = [sb(f"dst{u}", [L, TILES * TOP], I32) for u in range(2)]
        rows = [sb(f"rows{u}", [L, TOP, TILES, ROW]) for u in range(2)]
        top_val = sb("top_val", [L, B, TILES * TOP])
        share_sum = sb("share_sum", [L, B * TILES])
        filler = sb("filler", [P, ROW])
        fill_dst = sb("fill_dst", [P, E], I32)
        count_i = sb("count_i", [1, E], I32)
        tiles_i = sb("tiles_i", [1, E], I32)
        tiles_f = sb("tiles_f", [1, E])
        ones_e = sb("ones_e", [1, E])
        tiles_end = sb("tiles_end", [1, E])
        gated = sb("gated", [C, HTOK])
        hid = [sb(f"hid{u}", [C, HC, HTOK]) for u in range(2)]

        coef = hid[0][:].rearrange("p a b -> p (a b)")[:, 0:5 * C].rearrange("p (n c) -> p n c", n=5)
        proj_t = hid[1][:].rearrange("p a b -> p (a b)")[:, 0:4 * C].rearrange("p (n c) -> p n c", n=4)
        bits_s = q_dec[0][0:L, 0:BITS * (L + 1)].rearrange("p (n c) -> p n c", n=BITS)
        xg = [x_in[n // 7][:, n % 7 * ROW:(n % 7 + 1) * ROW] for n in range(8)]
        y_s = [x_in[1][:, 2 * ROW + n * C:2 * ROW + (n + 1) * C] for n in range(4)]
        xg_t = [q_t[0][:, n * P:(n + 1) * P] for n in range(2)]
        gate_e = [q_t[0][:, 2 * P + n * HID:2 * P + (n + 1) * HID] for n in range(2)]
        hid_e = [q_t[1][:, n * HID:(n + 1) * HID] for n in range(2)]
        hid_t = [q_dec[0][:, n * HID:(n + 1) * HID] for n in range(2)]
        slot_past = xn[0][0:1].rearrange("p a b -> p (a b)").bitcast(BF16)[:, 0:SLOTS * E].rearrange("p (t e) -> p t e", e=E)
        slot_tiles = xn[1][0:1].rearrange("p a b -> p (a b)").bitcast(BF16)[:, 0:SLOTS * E].rearrange("p (t e) -> p t e", e=E)
        slot_expert, slot_start = (prob[0][0:1, n * SLOTS:(n + 1) * SLOTS] for n in range(2))
        slot_row, slot_w = (prob[1][0:1, n * SLOTS:(n + 1) * SLOTS].bitcast(I32) for n in range(2))
        y_back = [[xn[u], xn_dec[u]] for u in range(2)]

        ps = [ctx.enter_context(nc.psum_tensor(f"bank{i}", [C, 512], F32)) for i in range(8)]
        P_H, P_TR, P_QR, P_G, P_O, P_A1, P_A3, P_S = ps
        P_T, P_A, P_HT, P_Y = (ps[0], ps[5]), (ps[1], ps[2]), (ps[3], ps[6]), (ps[4], ps[7])

        w_loaded = sem("w_loaded")
        proj_psum, proj_saved = sem("proj_psum"), sem("proj_saved")
        fold_psum, fold_saved = sem("fold_psum"), sem("fold_saved")
        dsig_ready, pw_step, mask_step, consts_ready = sem("dsig_ready"), sem("pw_step"), sem("mask_step"), sem("consts_ready")
        passed_dve, passed_pool = sem("passed_dve"), sem("passed_pool")
        half_set, iota_set = sem("half_set"), sem("iota_set")
        x_loaded = [sem(f"x_loaded{u}") for u in range(2)]
        h_psum, h_saved = sem("h_psum"), sem("h_saved")
        stat_done, mean_done, ve1_done, rstd1_ready = sem("stat_done"), sem("mean_done"), sem("ve1_done"), sem("rstd1_ready")
        xn_ready, xn_dec_ready = sem("xn_ready"), sem("xn_dec_ready")
        xn_t_psum, xn_t_ready = sem("xn_t_psum"), sem("xn_t_ready")
        q_psum, q_ready, q_dec_ready = sem("q_psum"), sem("q_ready"), sem("q_dec_ready")
        g_psum, state_step = sem("g_psum"), sem("state_step")
        s_psum, prob_ready = sem("s_psum"), sem("prob_ready")
        r_psum, ret_ready = sem("r_psum"), sem("ret_ready")
        o_psum, h2_ready = sem("o_psum"), sem("h2_ready")
        stat2_done, mean2_done, ve2_done, rstd2_ready = sem("stat2_done"), sem("mean2_done"), sem("ve2_done"), sem("rstd2_ready")
        xn2_ready = sem("xn2_ready")
        xn2_t_psum, xn2_t_ready = sem("xn2_t_psum"), sem("xn2_t_ready")
        gate_psum, gate_saved = sem("gate_psum"), sem("gate_saved")
        route_step, idx_ready, place_step = sem("route_step"), sem("idx_ready"), sem("place_step")
        a1_psum, a3_psum, gated_ready, hid_ready = sem("a1_psum"), sem("a3_psum"), sem("gated_ready"), sem("hid_ready")
        y_psum, y_added = sem("y_psum"), sem("y_added")
        xn2_copied, ids_ready = sem("xn2_copied"), sem("ids_ready")
        chosen_ready, place_psum, place_read, dst_ready = sem("chosen_ready"), sem("place_psum"), sem("place_read"), sem("dst_ready")
        rows_zeroed, filler_ready = sem("rows_zeroed"), sem("filler_ready")
        rows_sent = [sem(f"rows_sent{u}") for u in range(2)]
        spare_sent = sem("spare_sent")
        filler_sent, count_psum, table_step, table_ready, fill_dst_ready = sem("filler_sent"), sem("count_psum"), sem("table_step"), sem("table_ready"), sem("fill_dst_ready")
        share_sig, share_step, share_ready = sem("share_sig"), sem("share_step"), sem("share_ready")
        xg_loaded = [sem(f"xg_loaded{n}") for n in range(8)]
        y_sent = [sem(f"y_sent{n}") for n in range(8)]
        xg_t_psum, xg_t_ready, a_psum, gate_e_ready = sem("xg_t_psum"), sem("xg_t_ready"), sem("a_psum"), sem("gate_e_ready")
        hid_e_ready, hid_t_psum, hid_t_ready, ye_psum, ye_saved = sem("hid_e_ready"), sem("hid_t_psum"), sem("hid_t_ready"), sem("ye_psum"), sem("ye_saved")
        y_loaded = [sem(f"y_loaded{u}") for u in range(2)]
        first_added, both_added = sem("first_added"), sem("both_added")
        out_stored = sem("out_stored")

        HALVES = (1, 0)
        LOADS = 24
        block = ctx.enter_context(nc.Block())

        def stages(it, pair, u):
            def stage(lag):
                n = it - lag
                if isinstance(n, int) and not 0 <= n < B:
                    return None
                return n, (u - lag) % 2, pair + (u - lag) // 2
            return [stage(lag) for lag in range(5)]

        def steps(eng, step):
            for it in range(6):
                step(it, it // 2, it % 2)
            with eng.Fori(0, (B - 6) // 2) as i:
                for u in range(2):
                    step(i * 2 + (6 + u), i + 3, u)
            for it in range(B, B + 4):
                step(it, it // 2, it % 2)

        def slots(it, turn, n):
            def slot(lag):
                t = it - lag
                if isinstance(t, int) and not 0 <= t < SLOTS:
                    return None
                return t, (n - lag) % 8, turn + (n - lag) // 8
            return [slot(lag) for lag in range(4)]

        FIRST = 8 + (SLOTS % 8)

        def slot_steps(eng, step):
            for it in range(FIRST):
                step(it, it // 8, it % 8)
            with eng.Fori(0, (SLOTS - FIRST) // 8) as i:
                for n in range(8):
                    at = FIRST + n
                    step(i * 8 + at, i + at // 8, at % 8)
            for it in range(SLOTS, SLOTS + 3):
                step(it, it // 8, it % 8)

        @block.sync
        def _(sp):
            for to, src in ((w_tok_s[:], w_tok), (coef[:, 0, :], basis_t), (coef[:, 1, :], qc_t),
                            (coef[:, 2, :], kc_t), (coef[:, 3, :], vc_t), (coef[:, 4, :], oc_t),
                            (scal[:, 0:1], decay_logit), (scal[:, 1:2], out_scale),
                            (bits_s, exp_bits), (causal_s[:], causal), (ident_s[:], ident),
                            (gate_s[:], gate_t), (bias_s[:], biases), (before_f[:], before),
                            (pad_idx_s[:], pad_idx), (pad_dst_s[:], pad_dst), (region_s[:], region),
                            (fill_base_s[:], fill_base), (tile_no_s[:], tile_no)):
                sp.dma_start(to, src).then_inc(w_loaded, 16)

            def step(it, pair, u):
                s1 = stages(it, pair, u)[0]
                if s1:
                    b = s1[0]
                    if positive(2 * b - 2):
                        sp.wait_ge(h_psum, 2 * b - 2)
                    sp.dma_start(x_in[u][:], x_t[:, b, :]).then_inc(x_loaded[u], 16)
            steps(sp, step)

            sp.wait_ge(filler_ready, 1)
            for n in range(SPARE):
                sp.dma_start(routed[E * CAP + n * P:E * CAP + (n + 1) * P, :], filler[:]).then_inc(spare_sent, 16)
            for u in range(2):
                sp.wait_ge(rows_sent[u], 16 * TOP * TILES * B // 2)
            sp.wait_ge(spare_sent, 16 * SPARE)
            sp.wait_ge(filler_sent, 16 * E)
            sp.wait_ge(table_ready, 1)

            def slot_step(it, turn, n):
                s1 = slots(it, turn, n)[0]
                if s1:
                    t, v, used = s1
                    row = nc.sync.value_load(slot_row[0:1, bass.ds(t, 1)], min_val=0, max_val=ROWS - P)
                    if positive(used):
                        sp.wait_ge(y_sent[v], 16 * used)
                    sp.dma_start(xg[v], routed[bass.ds(row, P), :]).then_inc(xg_loaded[v], 16)
            slot_steps(sp, slot_step)

            for n in range(8):
                sp.wait_ge(y_sent[n], 16 * ((SLOTS - n + 7) // 8))
            full = (TILES - 1) * L

            def load_back(b, u, pair):
                if positive(b - 1):
                    sp.wait_ge(both_added, b - 1)
                for k in range(TOP):
                    at = b * PTOK + k * B * PTOK
                    sp.dma_start(y_back[u][k][:, 0:TILES - 1, :],
                                 results[bass.ds(at, full), :].rearrange("(j p) d -> p j d", p=L)).then_inc(y_loaded[u], 16)
                    sp.dma_start(y_back[u][k][0:REST, TILES - 1, :],
                                 results[bass.ds(at + full, REST), :]).then_inc(y_loaded[u], 16)
            for b in range(2):
                load_back(b, b, 0)
            with sp.Fori(1, B // 2) as i:
                for u in range(2):
                    load_back(i * 2 + u, u, i)

        @block.gpsimd
        def _(pool):
            nc.gpsimd.memset(half_neg[:], -0.5).then_inc(half_set, 1)
            nc.gpsimd.iota(iota_e[:], [[1, E]], base=0, channel_multiplier=0,
                           allow_small_or_imprecise_dtypes=True).then_inc(iota_set, 1)
            nc.gpsimd.memset(ones_s[:], 1.0).then_inc(iota_set, 1)
            nc.gpsimd.memset(ones_e[:], 1.0).then_inc(iota_set, 1)
            nc.gpsimd.memset(taken[:], 0.0).then_inc(iota_set, 1)
            nc.gpsimd.memset(filler[:], 0.0).then_inc(rows_zeroed, 1)
            for u in range(2):
                nc.gpsimd.memset(rows[u][:], 0.0).then_inc(rows_zeroed, 1)
            pool.wait_ge(rows_zeroed, 3)
            nc.gpsimd.iota(filler[:, C:C + 1].bitcast(I32), [[0, 1]], base=NOWHERE, channel_multiplier=0).then_inc(filler_ready, 1)
            for u in range(2):
                nc.gpsimd.iota(rows[u][:, :, :, C:C + 1].rearrange("p k j o -> p k (j o)").bitcast(I32),
                               [[B * PTOK, TOP], [L, TILES]], base=(u - 2) * PTOK, channel_multiplier=1).then_inc(filler_ready, 1)
            pool.wait_ge(half_set, 1)
            pool.wait_ge(consts_ready, 1)

            def step(it, pair, u):
                s1, _, s3, _, s5 = stages(it, pair, u)

                def send_rows(b, v, used, part):
                    if part == 0:
                        pool.wait_ge(dst_ready, b + 1)
                        pool.wait_ge(xn2_copied, 2 * b + 2)
                        pool.wait_ge(ids_ready, b + 1)
                        pool.sem_inc(passed_pool, 1)
                    for n in (range(0, 6), range(6, 11), range(11, 16))[part]:
                        j, k = n // TOP, n % TOP
                        nc.gpsimd.indirect_dma_start(routed, bass.IndirectOffsetOnAxis(dst[v][:, n:n + 1], 0),
                                                     rows[v][:, k, j, :], None, bounds_check=ROWS - 1,
                                                     oob_is_err=False).then_inc(rows_sent[v], 16)
                if s5:
                    send_rows(*s5, 0)
                if s1:
                    b = s1[0]
                    pool.wait_ge(mean_done, b + 1)
                    pool.sem_inc(passed_pool, 1)
                    nc.gpsimd.tensor_scalar(ve1[:], mv1[:, :, 1], EPS, None, ALU.add).then_inc(ve1_done, 1)
                    pool.wait_ge(ve1_done, b + 1)
                    nc.gpsimd.tensor_tensor(rstd1[:], ve1[:], half_neg[:], ALU.pow).then_inc(rstd1_ready, 1)
                if s5:
                    send_rows(*s5, 1)
                if s3:
                    b = s3[0]
                    pool.wait_ge(mean2_done, b + 1)
                    pool.sem_inc(passed_pool, 1)
                    nc.gpsimd.tensor_scalar(ve2[:], mv2[:, :, 1], EPS, None, ALU.add).then_inc(ve2_done, 1)
                    pool.wait_ge(ve2_done, b + 1)
                    nc.gpsimd.tensor_tensor(rstd2[:], ve2[:], half_neg[:], ALU.pow).then_inc(rstd2_ready, 1)
                if s5:
                    send_rows(*s5, 2)
            steps(pool, step)

            pool.wait_ge(filler_ready, 3)
            pool.wait_ge(fill_dst_ready, 1)
            for e in range(E):
                nc.gpsimd.indirect_dma_start(routed, bass.IndirectOffsetOnAxis(fill_dst[:, e:e + 1], 0), filler[:], None,
                                             bounds_check=ROWS - 1, oob_is_err=False).then_inc(filler_sent, 16)

            def slot_step(it, turn, n):
                s4 = slots(it, turn, n)[3]
                if s4:
                    t, v, used = s4
                    pool.wait_ge(ye_saved, t + 1)
                    pool.sem_inc(passed_pool, 1)
                    nc.gpsimd.indirect_dma_start(results, bass.IndirectOffsetOnAxis(xg[v][:, C:C + 1].bitcast(I32), 0),
                                                 y_s[v % 4], None, bounds_check=RESULTS - 1,
                                                 oob_is_err=False).then_inc(y_sent[v], 16)
            slot_steps(pool, slot_step)

        @block.scalar
        def _(act):
            for to, src in ((sw1_s[:], sw1), (sw3_s[:], sw3), (sw2_s[:], sw2), (w13_s[:], w13), (w2_s[:], w2)):
                act.dma_start(to, src).then_inc(w_loaded, 16)
            act.wait_ge(w_loaded, 16 * LOADS)
            nc.scalar.activation(powers[:, 0:1], scal[:, 0:1], ACT.Sigmoid).then_inc(dsig_ready, 1)
            act.wait_ge(proj_psum, 1)
            nc.scalar.copy(proj_t, P_H[:].rearrange("p (n c) -> p n c", n=4)).then_inc(proj_saved, 1)
            act.wait_ge(fold_psum, 1)
            nc.scalar.copy(wqk[:], P_TR[:, 0:C]).then_inc(fold_saved, 1)
            nc.scalar.activation(wvo[:], P_TR[:, C:2 * C], ACT.Copy, scale=scal[:, 1:2]).then_inc(fold_saved, 1)

            def step(it, pair, u):
                s1, s2, s3, s4, _ = stages(it, pair, u)

                def save_h(b, o):
                    act.wait_ge(h_psum, 2 * b + o + 1)
                    nc.scalar.copy(resid[:, b, o * 512:(o + 1) * 512], P_H[0:L, :]).then_inc(h_saved, 1)

                def save_xn_t(b, v, used, o):
                    hf = HALVES[o]
                    act.wait_ge(xn_t_psum, 2 * b + o + 1)
                    if positive(2 * b - 2):
                        act.wait_ge(s_psum, 2 * b - 2)
                    nc.scalar.copy(xn_t[v][:, hf * HTOK:(hf + 1) * HTOK], P_TR[:, 0:HTOK]).then_inc(xn_t_ready, 1)

                def save_ret(b, o):
                    hf = HALVES[o]
                    act.wait_ge(r_psum, 2 * b + o + 1)
                    if positive(2 * b):
                        act.wait_ge(o_psum, 2 * b)
                    nc.scalar.copy(ret_t[:, hf * HTOK:(hf + 1) * HTOK], P_QR[:, 0:HTOK]).then_inc(ret_ready, 1)

                def save_q(b, v, used, o):
                    hf = HALVES[o]
                    act.wait_ge(q_psum, 2 * b + o + 1)
                    if positive(2 * b - 2):
                        act.wait_ge(q_dec_ready, 2 * b - 2)
                    nc.scalar.copy(q_t[v][:, hf * HTOK:(hf + 1) * HTOK], P_QR[:, 0:HTOK]).then_inc(q_ready, 1)

                if s1:
                    save_h(s1[0], 0)
                if s2:
                    save_xn_t(*s2, 0)
                if s3:
                    save_ret(s3[0], 0)
                if s1:
                    save_h(s1[0], 1)
                if s2:
                    save_xn_t(*s2, 1)
                if s3:
                    save_ret(s3[0], 1)
                if s2:
                    save_q(*s2, 0)
                    save_q(*s2, 1)
                if s1:
                    b = s1[0]
                    act.wait_ge(xn_ready, b + 1)
                    if positive(2 * b - 2):
                        act.wait_ge(g_psum, 2 * b - 2)
                    nc.scalar.activation(xn_dec[u][:], xn[u][:], ACT.Copy, scale=mask[:, 0:1]).then_inc(xn_dec_ready, 1)
                if s4:
                    b, z, used = s4
                    for o in range(2):
                        hf = HALVES[o]
                        act.wait_ge(xn2_t_psum, 2 * b + o + 1)
                        if positive(b):
                            act.wait_ge(y_psum, 2 * b)
                            act.wait_ge(gate_psum, b)
                        nc.scalar.copy(xn2_t[:, hf * HTOK:(hf + 1) * HTOK], P_TR[:, 0:HTOK]).then_inc(xn2_t_ready, 1)
                    for n in range(2 * HC):
                        act.wait_ge(a1_psum, 2 * HC * b + n + 1)
                        if positive(2 * HC * b + n):
                            act.wait_ge(hid_ready, 2 * HC * b + n)
                        nc.scalar.activation(gated[:], P_A1[:, 0:HTOK], ACT.Silu).then_inc(gated_ready, 1)
                    act.wait_ge(xn2_ready, b + 1)
                    if positive(used):
                        act.wait_ge(rows_sent[z], 16 * TOP * TILES * used)
                    for k in range(TOP):
                        nc.scalar.copy(rows[z][:, k, :, 0:C], xn2[z][:]).then_inc(xn2_copied, 1)
            steps(act, step)

            act.wait_ge(route_step, 4 * B)
            nc.scalar.activation(top_val[:], top_val[:], ACT.Sigmoid).then_inc(share_sig, 1)

            def slot_step(it, turn, n):
                s1, s2, s3, _ = slots(it, turn, n)
                if s1:
                    t, v, used = s1
                    act.wait_ge(xg_t_psum, t + 1)
                    if positive(t - 1):
                        act.wait_ge(a_psum, t - 1)
                    nc.scalar.copy(xg_t[v % 2], P_T[v % 2][:, 0:P]).then_inc(xg_t_ready, 1)
                if s3:
                    t, v, used = s3
                    act.wait_ge(hid_t_psum, t + 1)
                    if positive(t - 1):
                        act.wait_ge(ye_psum, t - 1)
                    nc.scalar.copy(hid_t[v % 2], P_HT[v % 2][:, 0:HID]).then_inc(hid_t_ready, 1)
                if s2:
                    t, v, used = s2
                    act.wait_ge(a_psum, t + 1)
                    if positive(t - 1):
                        act.wait_ge(hid_e_ready, t - 1)
                    nc.scalar.activation(gate_e[v % 2], P_A[v % 2][:, 0:HID], ACT.Silu).then_inc(gate_e_ready, 1)
            slot_steps(act, slot_step)

            with act.Fori(0, B) as b:
                act.wait_ge(both_added, b + 1)
                act.dma_start(out[b, 0:(TILES - 1) * L, :].rearrange("(j p) d -> p j d", p=L),
                              resid[:, b, 0:(TILES - 1) * C].rearrange("p (j d) -> p j d", d=C)).then_inc(out_stored, 16)
                act.dma_start(out[b, (TILES - 1) * L:FRAMES, :],
                              resid[0:REST, b, (TILES - 1) * C:TILES * C]).then_inc(out_stored, 16)
            act.wait_ge(out_stored, 32 * B)

        @block.vector
        def _(dve):
            dve.wait_ge(dsig_ready, 1)
            nstep = 0
            for n in range(BITS - 1):
                nc.vector.tensor_tensor(powers[:, n + 1:n + 2], powers[:, n:n + 1], powers[:, n:n + 1], ALU.mult).then_inc(pw_step, 1)
                nstep += 1
                dve.wait_ge(pw_step, nstep)
            nc.vector.memset(decay_rev[:, C - 1:C], 1.0).then_inc(pw_step, 1)
            nstep += 1
            for n in range(BITS):
                dve.wait_ge(pw_step, nstep)
                w = 2 ** n
                nc.vector.tensor_scalar(decay_rev[:, C - 2 * w:C - w], decay_rev[:, C - w:C], powers[:, n:n + 1], None, ALU.mult).then_inc(pw_step, 1)
                nstep += 1
            dve.wait_ge(pw_step, nstep)
            nc.vector.tensor_copy(decay_len[:], decay_rev[:, C - 1 - L:C - L]).then_inc(pw_step, 1)
            nc.vector.tensor_copy(mask[:], causal_s[:]).then_inc(mask_step, 1)
            m = 1
            for n in range(BITS):
                dve.wait_ge(mask_step, m)
                nc.vector.tensor_scalar(factor[:], bits_s[:, n, :], -1.0, 1.0, ALU.mult, ALU.add).then_inc(mask_step, 1)
                dve.wait_ge(mask_step, m + 1)
                nc.vector.scalar_tensor_tensor(out=factor[:], in0=bits_s[:, n, :], scalar=powers[0:L, n:n + 1],
                                               in1=factor[:], op0=ALU.mult, op1=ALU.max).then_inc(mask_step, 1)
                dve.wait_ge(mask_step, m + 2)
                last = nc.vector.tensor_tensor(mask[:], mask[:], factor[:], ALU.mult)
                last.then_inc(mask_step, 1)
                m += 3
            dve.wait_ge(mask_step, m)
            dve.wait_ge(pw_step, nstep + 1)
            nc.vector.tensor_scalar(factor[:, 0:1], mask[:, 0:1], 1.0, None, ALU.mult).then_inc(consts_ready, 1)
            dve.wait_ge(iota_set, 4)
            dve.wait_ge(filler_ready, 3)
            nc.vector.tensor_copy(before_s[:], before_f[:]).then_inc(consts_ready, 1)

            def means(b, src, done, aggregated, mv, count):
                dve.sem_inc(passed_dve, 1)
                for t in range(TILES):
                    last = nc.vector.bn_stats(stats[:, t, :], src[:, t * C:(t + 1) * C])
                last.then_inc(done, 1)
                dve.wait_ge(done, count + 1)
                dve.sem_inc(passed_dve, 1)
                for t in range(TILES):
                    last = nc.vector.bn_aggr(mv[:, t, :], stats[:, t, :])
                last.then_inc(aggregated, 1)

            def step(it, pair, u):
                s1, s2, s3, s4, _ = stages(it, pair, u)
                if s1:
                    b = s1[0]
                    dve.wait_ge(h_saved, 2 * b + 2)
                    if positive(b):
                        dve.wait_ge(rstd1_ready, b)
                    means(b, resid[:, b, :], stat_done, mean_done, mv1, b)
                for o in range(2):
                    hf = HALVES[o]
                    if s2:
                        b, v, _ = s2
                        cols = slice(hf * HTOK, (hf + 1) * HTOK)
                        dve.wait_ge(q_ready, 2 * b + o + 1)
                        if positive(2 * b - 2):
                            dve.wait_ge(r_psum, 2 * b - 2)
                        nc.vector.tensor_tensor(q_dec[v][:, cols].rearrange("p (j t) -> p j t", t=L),
                                                q_t[v][:, cols].rearrange("p (j t) -> p j t", t=L),
                                                decay_rev[:, C - L:C].unsqueeze(1).to_broadcast([C, HT, L]),
                                                ALU.mult).then_inc(q_dec_ready, 1)
                    if s3:
                        b, w, _ = s3
                        dve.wait_ge(o_psum, 2 * b + o + 1)
                        part = resid[:, b, hf * 512:(hf + 1) * 512]
                        nc.vector.tensor_tensor(part, P_O[0:L, :], part, ALU.add).then_inc(h2_ready, 1)
                if s3:
                    b, w, _ = s3
                    dve.wait_ge(h2_ready, 2 * b + 2)
                    means(b, resid[:, b, :], stat2_done, mean2_done, mv2, b)
                if s2:
                    b, v, _ = s2
                    if positive(2 * b - 2):
                        dve.wait_ge(r_psum, 2 * b - 2)
                    for o in range(2):
                        hf = HALVES[o]
                        dve.wait_ge(g_psum, 2 * b + o + 1)
                        for n, c in enumerate((7, 6, 5, 4) if hf else (3, 2, 1)):
                            part = P_G[:, n * C:(n + 1) * C]
                            if c == TILES - 1:
                                nc.vector.tensor_copy(state[v][:, c - 1, :], part).then_inc(state_step, 1)
                            else:
                                dve.wait_ge(state_step, 7 * b + (7 - c))
                                nc.vector.scalar_tensor_tensor(out=state[v][:, c - 1, :], in0=state[v][:, c, :],
                                                               scalar=decay_len[:, 0:1], in1=part,
                                                               op0=ALU.mult, op1=ALU.add).then_inc(state_step, 1)
                        dve.wait_ge(s_psum, 2 * b + o + 1)
                        cols = slice(hf * HTOK, (hf + 1) * HTOK)
                        nc.vector.tensor_tensor(prob[v][:, cols].rearrange("p (j t) -> p j t", t=L),
                                                P_S[0:L, 0:HTOK].rearrange("p (j t) -> p j t", t=L),
                                                mask[:, 1:L + 1].unsqueeze(1).to_broadcast([L, HT, L]),
                                                ALU.mult).then_inc(prob_ready, 1)
                if s1:
                    b = s1[0]
                    dve.wait_ge(rstd1_ready, b + 1)
                    if positive(2 * b - 2):
                        dve.wait_ge(r_psum, 2 * b - 2)
                    if positive(b - 1):
                        dve.wait_ge(xn_dec_ready, b - 1)
                    for t in range(TILES):
                        last = nc.vector.tensor_scalar(xn[u][:, t, :], resid[:, b, t * C:(t + 1) * C],
                                                       mv1[:, t, 0:1], rstd1[:, t:t + 1], ALU.subtract, ALU.mult)
                    last.then_inc(xn_ready, 1)
                if s3:
                    b, w, _ = s3
                    dve.wait_ge(rstd2_ready, b + 1)
                    if positive(2 * b - 2):
                        dve.wait_ge(xn2_t_psum, 2 * b - 2)
                        dve.wait_ge(xn2_copied, 2 * b - 2)
                    for t in range(TILES):
                        last = nc.vector.tensor_scalar(xn2[w][:, t, :], resid[:, b, t * C:(t + 1) * C],
                                                       mv2[:, t, 0:1], rstd2[:, t:t + 1], ALU.subtract, ALU.mult)
                    last.then_inc(xn2_ready, 1)
                if s4:
                    b, z, used = s4
                    dve.wait_ge(gate_psum, b + 1)
                    nc.vector.tensor_copy(raw[:].rearrange("p j e -> p (j e)"), P_O[0:L, 0:TILES * E]).then_inc(route_step, 1)
                    nc.vector.tensor_tensor(biased[:], P_O[0:L, 0:TILES * E].rearrange("p (j e) -> p j e", e=E),
                                            bias_s[0:L, :].unsqueeze(1).to_broadcast([L, TILES, E]), ALU.add).then_inc(gate_saved, 1)
                    dve.wait_ge(route_step, 4 * b + 1)
                    dve.wait_ge(gate_saved, b + 1)
                    dve.sem_inc(passed_dve, 1)
                    for t in range(TILES):
                        nc.vector.max(top_biased[:, t, :], biased[:, t, :])
                        last = nc.vector.max(top_raw[:, t, :], raw[:, t, :])
                    last.then_inc(route_step, 1)
                    dve.wait_ge(route_step, 4 * b + 2)
                    dve.sem_inc(passed_dve, 1)
                    for t in range(TILES):
                        last = nc.vector.max_index(top_idx[:, t, :], top_biased[:, t, :], biased[:, t, :])
                    last.then_inc(route_step, 1)
                    nc.vector.tensor_copy(top_val[:, b, :].rearrange("p (j k) -> p j k", k=TOP), top_raw[:, :, 0:TOP]).then_inc(route_step, 1)
                    dve.wait_ge(route_step, 4 * b + 4)
                    nc.vector.tensor_tensor(idx_f[:].rearrange("p (j k) -> p j k", k=TOP), top_idx[:, :, 0:TOP],
                                            pad_idx_s[:].rearrange("p (j k) -> p j k", k=TOP), ALU.add).then_inc(idx_ready, 1)
                    dve.wait_ge(idx_ready, b + 1)
                    nc.vector.tensor_tensor(chosen[:].rearrange("p j k e -> p (j k) e"),
                                            iota_e[:].unsqueeze(1).to_broadcast([L, TILES * TOP, E]),
                                            idx_f[:].unsqueeze(2).to_broadcast([L, TILES * TOP, E]), ALU.is_equal).then_inc(chosen_ready, 1)
                    dve.wait_ge(chosen_ready, 2 * b + 1)
                    nc.vector.tensor_tensor(assigned[:], chosen[:, :, 0, :], chosen[:, :, 1, :], ALU.add).then_inc(chosen_ready, 1)
                    n = 0
                    for o in range(2):
                        hf = HALVES[o]
                        for hc in range(HC):
                            g = 2 * HC * b + n
                            dve.wait_ge(gated_ready, g + 1)
                            dve.wait_ge(a3_psum, g + 1)
                            if positive(2 * b + o - 1):
                                dve.wait_ge(y_psum, 2 * b + o - 1)
                            nc.vector.tensor_tensor(hid[o][:, hc, :], gated[:], P_A3[:, 0:HTOK], ALU.mult).then_inc(hid_ready, 1)
                            n += 1
                        dve.wait_ge(y_psum, 2 * b + o + 1)
                        part = resid[:, b, hf * 512:(hf + 1) * 512]
                        nc.vector.tensor_tensor(part, P_O[0:L, :], part, ALU.add).then_inc(y_added, 1)
                    dve.wait_ge(place_psum, b + 1)
                    nc.vector.tensor_tensor(place[:], P_O[0:L, 0:TILES * E].rearrange("p (j e) -> p j e", e=E),
                                            region_s[:].unsqueeze(1).to_broadcast([L, TILES, E]), ALU.add).then_inc(place_read, 1)
                    nc.vector.tensor_reduce(assigned_sum[:], assigned[:].rearrange("p j e -> p e j"), AX.X, ALU.add).then_inc(place_step, 1)
                    dve.wait_ge(place_step, 4 * b + 1)
                    dve.wait_ge(place_read, b + 1)
                    nc.vector.tensor_tensor(taken[:], taken[:], assigned_sum[:], ALU.add).then_inc(place_step, 1)
                    nc.vector.tensor_tensor(chosen_place[:].rearrange("p (j k) e -> p j k e", k=TOP), chosen[:],
                                            place[:].unsqueeze(2).to_broadcast([L, TILES, TOP, E]), ALU.mult).then_inc(place_step, 1)
                    dve.wait_ge(place_step, 4 * b + 3)
                    nc.vector.tensor_reduce(place_sum[:], chosen_place[:], AX.X, ALU.add).then_inc(place_step, 1)
                    if positive(used):
                        dve.wait_ge(rows_sent[z], 16 * TOP * TILES * used)
                    dve.wait_ge(place_step, 4 * b + 4)
                    nc.vector.tensor_tensor(dst[z][:], place_sum[:], pad_dst_s[:], ALU.add).then_inc(dst_ready, 1)
                    ids = rows[z][:, :, :, C:C + 1].rearrange("p k j o -> p k (j o)").bitcast(I32)
                    nc.vector.tensor_scalar(ids, ids, 2.0 * PTOK, None, ALU.add).then_inc(ids_ready, 1)
            steps(dve, step)

            dve.wait_ge(count_psum, 1)
            nc.vector.tensor_tensor(fill_dst[:], P_O[:, 0:E], fill_base_s[:], ALU.add).then_inc(fill_dst_ready, 1)
            nc.vector.tensor_scalar(count_i[:], P_O[0:1, 0:E], P - 1.0, None, ALU.add).then_inc(table_step, 1)
            dve.wait_ge(table_step, 1)
            nc.vector.tensor_scalar(tiles_i[:], count_i[:], 7, None, ALU.logical_shift_right).then_inc(table_step, 1)
            dve.wait_ge(table_step, 2)
            nc.vector.tensor_copy(tiles_f[:], tiles_i[:]).then_inc(table_step, 1)
            dve.wait_ge(table_step, 3)
            nc.vector.tensor_tensor_scan(tiles_end[:], ones_e[:], tiles_f[:], 0.0, ALU.mult, ALU.add).then_inc(table_step, 1)
            dve.wait_ge(table_step, 4)
            dve.wait_ge(xn_dec_ready, B)
            dve.wait_ge(r_psum, 2 * B)
            nc.vector.tensor_tensor(slot_past, tiles_end[:].unsqueeze(1).to_broadcast([1, SLOTS, E]),
                                    tile_no_s[:, 0, :].unsqueeze(2).to_broadcast([1, SLOTS, E]), ALU.is_le).then_inc(table_step, 1)
            dve.wait_ge(table_step, 5)
            nc.vector.tensor_tensor(slot_tiles, slot_past, tiles_f[:].unsqueeze(1).to_broadcast([1, SLOTS, E]), ALU.mult).then_inc(table_step, 1)
            nc.vector.tensor_reduce(slot_expert[:], slot_past, AX.X, ALU.add).then_inc(table_step, 1)
            dve.wait_ge(table_step, 7)
            nc.vector.tensor_reduce(slot_start[:], slot_tiles, AX.X, ALU.add).then_inc(table_step, 1)
            dve.wait_ge(table_step, 8)
            nc.vector.scalar_tensor_tensor(out=slot_start[:], in0=slot_start[:], scalar=-float(P), in1=tile_no_s[:, 1, :],
                                           op0=ALU.mult, op1=ALU.add).then_inc(table_step, 1)
            dve.wait_ge(table_step, 9)
            nc.vector.scalar_tensor_tensor(out=slot_row[:], in0=slot_expert[:], scalar=float(CAP), in1=slot_start[:],
                                           op0=ALU.mult, op1=ALU.add)
            nc.vector.tensor_scalar(slot_w[:], slot_expert[:], E - 1.0, None, ALU.min).then_inc(table_ready, 1)

            dve.wait_ge(share_sig, 1)
            both = top_val[:].rearrange("p b (j k) -> p (b j) k", k=TOP)
            nc.vector.tensor_reduce(share_sum[:], both, AX.X, ALU.add).then_inc(share_step, 1)
            dve.wait_ge(share_step, 1)
            nc.vector.reciprocal(share_sum[:], share_sum[:]).then_inc(share_step, 1)
            dve.wait_ge(share_step, 2)
            nc.vector.tensor_tensor(both, both, share_sum[:].unsqueeze(2).to_broadcast([L, B * TILES, TOP]), ALU.mult).then_inc(share_ready, 1)

            def slot_step(it, turn, n):
                _, s2, _, s4 = slots(it, turn, n)
                if s4:
                    t, v, used = s4
                    dve.wait_ge(ye_psum, t + 1)
                    if positive(used - 1 + v // 4):
                        dve.wait_ge(y_sent[(v - 4) % 8], 16 * (used + v // 4))
                    elif v >= 4:
                        dve.wait_ge(y_sent[v - 4], 16)
                    nc.vector.tensor_copy(y_s[v % 4], P_Y[v % 2][:, 0:C]).then_inc(ye_saved, 1)
                if s2:
                    t, v, used = s2
                    dve.wait_ge(gate_e_ready, t + 1)
                    if positive(t - 1):
                        dve.wait_ge(hid_t_psum, t - 1)
                    nc.vector.tensor_tensor(hid_e[v % 2], gate_e[v % 2], P_A[v % 2][:, HID:2 * HID], ALU.mult).then_inc(hid_e_ready, 1)
            slot_steps(dve, slot_step)

            dve.wait_ge(share_ready, 1)

            def add_back(b, u, used):
                dve.wait_ge(y_loaded[u], 64 * used + 64)
                for k in range(TOP):
                    if k:
                        dve.wait_ge(first_added, b + 1)
                    for t in range(TILES):
                        n = L if t < TILES - 1 else REST
                        part = resid[0:n, b, t * C:(t + 1) * C]
                        last = nc.vector.scalar_tensor_tensor(out=part, in0=y_back[u][k][0:n, t, :],
                                                              scalar=top_val[0:n, b, TOP * t + k:TOP * t + k + 1],
                                                              in1=part, op0=ALU.mult, op1=ALU.add)
                    last.then_inc(both_added if k else first_added, 1)
            with dve.Fori(0, B // 2) as i:
                for u in range(2):
                    add_back(i * 2 + u, u, i)

        @block.tensor
        def _(pe):
            pe.wait_ge(w_loaded, 16 * LOADS)
            pe.wait_ge(consts_ready, 2)
            pe.wait_ge(iota_set, 4)
            for n in range(4):
                last = nc.tensor.matmul(P_H[:, n * C:(n + 1) * C], coef[:, n + 1, :], coef[:, 0, :], start=True, stop=True)
            last.then_inc(proj_psum, 1)
            pe.wait_ge(proj_saved, 1)
            nc.tensor.matmul(P_TR[:, 0:C], proj_t[:, 0, :], proj_t[:, 1, :], start=True, stop=True)
            nc.tensor.matmul(P_TR[:, C:2 * C], proj_t[:, 2, :], proj_t[:, 3, :], start=True, stop=True).then_inc(fold_psum, 1)
            pe.wait_ge(fold_saved, 2)

            def step(it, pair, u):
                s1, s2, s3, s4, _ = stages(it, pair, u)

                def tokens(b, o):
                    if o == 0:
                        pe.wait_ge(x_loaded[u], 16 * pair + 16)
                    if positive(2 * b + o):
                        pe.wait_ge(h_saved, 2 * b + o)
                    for j in range(HT):
                        m = (HT * o + j) * L
                        nc.tensor.matmul(P_H[0:L, j * C:(j + 1) * C], x_in[u][:, m:m + L], w_tok_s[:, 0, :], start=True, stop=False)
                        last = nc.tensor.matmul(P_H[0:L, j * C:(j + 1) * C], x_in[u][:, m + 1:m + 1 + L], w_tok_s[:, 1, :], start=False, stop=True)
                    last.then_inc(h_psum, 1)

                def turn(b, v, used, o):
                    if o == 0:
                        pe.wait_ge(xn_ready, b + 1)
                    if positive(2 * b + o):
                        pe.wait_ge(xn_t_ready, 2 * b + o)
                    if positive(2 * b - 4):
                        pe.wait_ge(xn2_t_ready, 2 * b - 4)
                    for j in range(HT):
                        last = nc.tensor.transpose(P_TR[:, j * L:(j + 1) * L], xn[v][:, HT * HALVES[o] + j, :], ident_s[0:L, 0:L])
                    last.then_inc(xn_t_psum, 1)

                def retrieve(b, w, used, o):
                    if o == 0:
                        pe.wait_ge(prob_ready, 2 * b + 2)
                        pe.wait_ge(state_step, 7 * b + 7)
                        pe.wait_ge(q_dec_ready, 2 * b + 2)
                        pe.wait_ge(q_ready, 2 * b + 2)
                    if positive(2 * b + o):
                        pe.wait_ge(ret_ready, 2 * b + o)
                    for j in range(HT):
                        c = HT * HALVES[o] + j
                        tok = slice(c * L, (c + 1) * L)
                        dst = P_QR[:, j * L:(j + 1) * L]
                        last = nc.tensor.matmul(dst, xn[w][:, c, :], prob[w][:, tok], start=True, stop=(c == TILES - 1))
                        if c < TILES - 1:
                            last = nc.tensor.matmul(dst, state[w][:, c, :], q_dec[w][:, tok], start=False, stop=True)
                    last.then_inc(r_psum, 1)

                def queries(b, v, used, o):
                    pe.wait_ge(xn_t_ready, 2 * b + o + 1)
                    if positive(2 * b + o):
                        pe.wait_ge(q_ready, 2 * b + o)
                    if positive(2 * b):
                        pe.wait_ge(ret_ready, 2 * b)
                    cols = slice(HALVES[o] * HTOK, (HALVES[o] + 1) * HTOK)
                    nc.tensor.matmul(P_QR[:, 0:HTOK], wqk[:], xn_t[v][:, cols], start=True, stop=True).then_inc(q_psum, 1)

                def project(b, o):
                    pe.wait_ge(ret_ready, 2 * b + o + 1)
                    if positive(2 * b + o):
                        pe.wait_ge(h2_ready, 2 * b + o)
                    if positive(b - 1):
                        pe.wait_ge(place_read, b - 1)
                    for j in range(HT):
                        c = HT * HALVES[o] + j
                        last = nc.tensor.matmul(P_O[0:L, j * C:(j + 1) * C], ret_t[:, c * L:(c + 1) * L], wvo[:], start=True, stop=True)
                    last.then_inc(o_psum, 1)

                def keys(b, v, used, o):
                    if o == 0:
                        pe.wait_ge(xn_dec_ready, b + 1)
                    if positive(7 * b + 4 * o):
                        pe.wait_ge(state_step, 7 * b + 4 * o)
                    for n, c in enumerate((3, 2, 1) if o else (7, 6, 5, 4)):
                        last = nc.tensor.matmul(P_G[:, n * C:(n + 1) * C], xn_dec[v][:, c, :], xn[v][:, c, :], start=True, stop=True)
                    last.then_inc(g_psum, 1)

                def scores(b, v, used, o):
                    pe.wait_ge(q_ready, 2 * b + o + 1)
                    if positive(2 * b + o):
                        pe.wait_ge(prob_ready, 2 * b + o)
                    for j in range(HT):
                        c = HT * HALVES[o] + j
                        tok = slice(c * L, (c + 1) * L)
                        last = nc.tensor.matmul(P_S[0:L, j * L:(j + 1) * L], xn_t[v][:, tok], q_t[v][:, tok], start=True, stop=True)
                    last.then_inc(s_psum, 1)

                if s1:
                    tokens(s1[0], 0)
                if s2:
                    turn(*s2, 0)
                if s3:
                    retrieve(*s3, 0)
                if s1:
                    tokens(s1[0], 1)
                if s2:
                    turn(*s2, 1)
                if s3:
                    retrieve(*s3, 1)
                if s2:
                    queries(*s2, 0)
                if s3:
                    project(s3[0], 0)
                if s2:
                    queries(*s2, 1)
                if s3:
                    project(s3[0], 1)
                if s2:
                    keys(*s2, 0)
                    scores(*s2, 0)
                    keys(*s2, 1)
                    scores(*s2, 1)
                if s4:
                    b, z, _ = s4
                    for o in range(2):
                        if o == 0:
                            pe.wait_ge(xn2_ready, b + 1)
                        if positive(2 * b + o):
                            pe.wait_ge(xn2_t_ready, 2 * b + o)
                        pe.wait_ge(xn_t_ready, cap(2 * b + 6, 2 * B))
                        for j in range(HT):
                            last = nc.tensor.transpose(P_TR[:, j * L:(j + 1) * L], xn2[z][:, HT * HALVES[o] + j, :], ident_s[0:L, 0:L])
                        last.then_inc(xn2_t_psum, 1)
                    pe.wait_ge(xn2_t_ready, 2 * b + 2)
                    pe.wait_ge(h2_ready, cap(2 * b + 4, 2 * B))
                    if positive(b):
                        pe.wait_ge(place_read, b)
                    for c in range(TILES):
                        last = nc.tensor.matmul(P_O[0:L, c * E:(c + 1) * E], xn2_t[:, c * L:(c + 1) * L], gate_s[:], start=True, stop=True)
                    last.then_inc(gate_psum, 1)
                    n = 0
                    for o in range(2):
                        cols = slice(HALVES[o] * HTOK, (HALVES[o] + 1) * HTOK)
                        for hc in range(HC):
                            g = 2 * HC * b + n
                            if positive(g):
                                pe.wait_ge(gated_ready, g)
                            nc.tensor.matmul(P_A1[:, 0:HTOK], sw1_s[:, hc * C:(hc + 1) * C], xn2_t[:, cols], start=True, stop=True).then_inc(a1_psum, 1)
                            if positive(g):
                                pe.wait_ge(hid_ready, g)
                            nc.tensor.matmul(P_A3[:, 0:HTOK], sw3_s[:, hc * C:(hc + 1) * C], xn2_t[:, cols], start=True, stop=True).then_inc(a3_psum, 1)
                            n += 1
                        pe.wait_ge(hid_ready, 2 * HC * b + n)
                        pe.wait_ge(gate_saved, b + 1)
                        if positive(2 * b + o):
                            pe.wait_ge(y_added, 2 * b + o)
                        for j in range(HT):
                            for hc in range(HC):
                                last = nc.tensor.matmul(P_O[0:L, j * C:(j + 1) * C], hid[o][:, hc, j * L:(j + 1) * L], sw2_s[:, hc, :],
                                                        start=(hc == 0), stop=(hc == HC - 1))
                        last.then_inc(y_psum, 1)
                    pe.wait_ge(chosen_ready, 2 * b + 2)
                    pe.wait_ge(y_added, 2 * b + 2)
                    if positive(b):
                        pe.wait_ge(place_step, 4 * b)
                    nc.tensor.matmul(P_O[0:L, 0:TILES * E], before_s[:], assigned[:].rearrange("p j e -> p (j e)"), start=True, stop=False)
                    nc.tensor.matmul(P_O[0:L, 0:TILES * E], ones_s[:, 0:L], taken[:].unsqueeze(1).to_broadcast([L, TILES, E]), start=False, stop=False)
                    for j in range(TILES - 1):
                        last = nc.tensor.matmul(P_O[0:L, (j + 1) * E:TILES * E], ones_s[:, 0:L],
                                                assigned[:, j:j + 1, :].to_broadcast([L, TILES - 1 - j, E]),
                                                start=False, stop=(j == TILES - 2))
                    last.then_inc(place_psum, 1)
            steps(pe, step)

            pe.wait_ge(place_step, 4 * B)
            pe.wait_ge(place_read, B)
            nc.tensor.matmul(P_O[:, 0:E], ones_s[:], taken[:], start=True, stop=True).then_inc(count_psum, 1)
            pe.wait_ge(table_ready, 1)

            def slot_step(it, turn, n):
                s1, s2, s3, s4 = slots(it, turn, n)
                if s4:
                    we4 = nc.tensor.value_load(slot_w[0:1, bass.ds(s4[0], 1)], min_val=0, max_val=E - 1)
                if s2:
                    we2 = nc.tensor.value_load(slot_w[0:1, bass.ds(s2[0], 1)], min_val=0, max_val=E - 1)
                if s1:
                    t, v, used = s1
                    pe.wait_ge(xg_loaded[v], 16 * used + 16)
                    if positive(t - 1):
                        pe.wait_ge(xg_t_ready, t - 1)
                    nc.tensor.transpose(P_T[v % 2][:, 0:P], xg[v][:, 0:C], ident_s[:]).then_inc(xg_t_psum, 1)
                if s3:
                    t, v, used = s3
                    pe.wait_ge(hid_e_ready, t + 1)
                    if positive(t - 1):
                        pe.wait_ge(hid_t_ready, t - 1)
                    for hc in range(HC):
                        last = nc.tensor.transpose(P_HT[v % 2][:, hc * C:(hc + 1) * C], hid_e[v % 2][:, hc * C:(hc + 1) * C], ident_s[:])
                    last.then_inc(hid_t_psum, 1)
                if s2:
                    t, v, used = s2
                    pe.wait_ge(xg_t_ready, t + 1)
                    if positive(t - 1):
                        pe.wait_ge(hid_e_ready, t - 1)
                    nc.tensor.matmul(P_A[v % 2][:], xg_t[v % 2], w13_s[:, bass.ds(we2 * (2 * HID), 2 * HID)], start=True, stop=True).then_inc(a_psum, 1)
                if s4:
                    t, v, used = s4
                    pe.wait_ge(hid_t_ready, t + 1)
                    if positive(t - 1):
                        pe.wait_ge(ye_saved, t - 1)
                    for hc in range(HC):
                        last = nc.tensor.matmul(P_Y[v % 2][:, 0:C], hid_t[v % 2][:, hc * C:(hc + 1) * C],
                                                w2_s[:, bass.ds(we4 * (HC * C) + hc * C, C)], start=(hc == 0), stop=(hc == HC - 1))
                    last.then_inc(ye_psum, 1)
            slot_steps(pe, slot_step)


def constants():
    n = np.arange(2 * C, dtype=np.float64) + 0.5
    cosine = np.float32(np.sqrt(4.0 / C) * np.cos(np.outer(n + C / 2, np.pi / C * n[:C]))).astype(np.float64)
    window = np.float32(np.sin(np.pi * n / (2 * C))).astype(np.float64)
    w_tok = (window[:, None] * cosine).astype(np.float32).reshape(2, C, C).transpose(1, 0, 2)
    s, t = np.arange(L)[:, None], np.arange(-1, L)[None, :]
    expo = np.maximum(s - t - 1, 0)
    bits = (expo[:, None, :] >> np.arange(BITS)[None, :, None] & 1).astype(np.float32)
    pad = np.zeros((L, TILES, TOP), np.float32)
    pad[REST:, TILES - 1, :] = 1
    pad = pad.reshape(L, TILES * TOP)
    e = np.arange(E)[None, :]
    tile = np.arange(SLOTS)
    route = {"before": (np.arange(L)[:, None] < np.arange(L)[None, :]).astype(np.float32),
             "pad_idx": pad * (2 * E), "pad_dst": pad * NOWHERE,
             "region": np.repeat(e * CAP, L, 0).astype(np.float32),
             "fill_base": (e * CAP + np.arange(P)[:, None]).astype(np.float32),
             "tile_no": np.stack([tile, P * tile])[None].astype(np.float32)}
    return route | {"w_tok": np.ascontiguousarray(w_tok), "exp_bits": bits,
            "causal": (s > t).astype(np.float32), "ident": np.eye(C, dtype=np.float32)}


def kernel(x, L0_attn_basis, L0_attn_q_coeffs, L0_attn_k_coeffs, L0_attn_v_coeffs, L0_attn_o_coeffs,
           L0_attn_decay_logit, L0_attn_out_scale, L0_ffn_gate_w, L0_ffn_biases, L0_ffn_w1, L0_ffn_w3,
           L0_ffn_w2, L0_ffn_sw1, L0_ffn_sw3, L0_ffn_sw2):
    import concourse.bacc as bacc
    from concourse.bass_utils import run_bass_kernel_spmd

    f = np.float32
    padded = np.zeros((B, CHUNKS * C), f)
    padded[:, C:C + SAMPLES] = x
    t = lambda a: np.ascontiguousarray(np.asarray(a).T)
    arrays = constants() | {
        "x_t": np.ascontiguousarray(padded.reshape(B, CHUNKS, C).transpose(2, 0, 1)),
        "basis_t": t(L0_attn_basis), "qc_t": t(L0_attn_q_coeffs), "kc_t": t(L0_attn_k_coeffs),
        "vc_t": t(L0_attn_v_coeffs), "oc_t": t(L0_attn_o_coeffs),
        "decay_logit": np.broadcast_to(np.asarray(L0_attn_decay_logit).reshape(1, 1), (C, 1)).copy(),
        "out_scale": np.broadcast_to(np.asarray(L0_attn_out_scale).reshape(1, 1), (C, 1)).copy(),
        "gate_t": t(L0_ffn_gate_w),
        "biases": np.broadcast_to(np.asarray(L0_ffn_biases)[None, :], (C, E)).copy(),
        "w13": np.concatenate([L0_ffn_w1, L0_ffn_w3], axis=2).transpose(1, 0, 2).reshape(C, E * 2 * HID).copy(),
        "w2": np.asarray(L0_ffn_w2).reshape(E, HC, C, C).transpose(2, 0, 1, 3).reshape(C, E * HC * C).copy(),
        "sw1": np.asarray(L0_ffn_sw1), "sw3": np.asarray(L0_ffn_sw3),
        "sw2": np.asarray(L0_ffn_sw2).reshape(HC, C, C).transpose(1, 0, 2).copy(),
    }
    names = ["x_t", "w_tok", "basis_t", "qc_t", "kc_t", "vc_t", "oc_t", "decay_logit", "out_scale", "gate_t",
             "biases", "w13", "w2", "sw1", "sw3", "sw2", "exp_bits", "causal", "ident", "before", "pad_idx", "pad_dst",
             "region", "fill_base", "tile_no"]
    nc = bacc.Bacc("TRN2", target_bir_lowering=False, num_devices=1)
    args = [nc.dram_tensor(n, arrays[n].shape, mybir.dt.from_np(arrays[n].dtype), kind="ExternalInput").ap() for n in names]
    out = nc.dram_tensor("out", (B, FRAMES, C), F32, kind="ExternalOutput").ap()
    routed = nc.dram_tensor("routed", (ROWS, ROW), F32, kind="Internal").ap()
    results = nc.dram_tensor("results", (RESULTS, C), F32, kind="Internal").ap()
    audio_tower(nc, *args, routed, results, out)
    r = run_bass_kernel_spmd(nc, [arrays], core_ids=[0])
    return r.results[0]["out"]
```

```python
from contextlib import ExitStack

import numpy as np

import concourse.bass as bass
from concourse import mybir

F32 = mybir.dt.float32
BF16 = mybir.dt.bfloat16
F16 = mybir.dt.float16
I32 = mybir.dt.int32
U32 = mybir.dt.uint32
ALU = mybir.AluOpType
ACT = mybir.ActivationFunctionType
AX = mybir.AxisListType

B = 16
SAMPLES = 120000
C = 128
FRAMES = 939
L = 120
TILES = 8
HT = TILES // 2
HTOK = HT * L
PTOK = TILES * L
REST = FRAMES - (TILES - 1) * L
CHUNKS = PTOK + 1
HID = 256
HC = HID // C
E = 8
BITS = 7
EPS = 1e-5
TOP = 2
P = 128
SUB = 2
R = SUB * P
ROW = C + 4
CAP = B * PTOK + R
EARLY = 10
SLOTS = (TOP * B * FRAMES + E * (R - 1)) // R
EARLY_SLOTS = (TOP * EARLY * FRAMES + E * (R - 1)) // R
ONLY_EARLY = -(-TOP * EARLY * FRAMES // R)
SPARE = SLOTS - -(-TOP * B * FRAMES // R)
ROWS = E * CAP + SPARE * R
RING = 8
BACK = 4
YS = 4
BACK_TURN = -(-(EARLY_SLOTS - 1) // RING) + 1
TURNS = SLOTS // RING
ADDED = 2 * (TURNS - BACK_TURN)
ENDS = 2 * E + 1
LEAD = 4
TABLE = -(-(SLOTS + LEAD) // 4) * 4 + 4
RESULTS = TOP * B * PTOK
NOWHERE = 1 << 20


def positive(n):
    return not isinstance(n, int) or n > 0


def cap(n, top):
    return min(n, top) if isinstance(n, int) else n


def audio_tower(nc, x_t, tok_ident, coefs_t, small, exp_bits, masks, route, tiles, sw13, sw2, w13, w2,
                routed, results, out):
    with ExitStack() as ctx:
        def sb(name, shape, dt=F32):
            return ctx.enter_context(nc.sbuf_tensor(name, shape, dt))

        def sem(name):
            return ctx.enter_context(nc.semaphore(name))

        wqk = sb("wqk", [C, C])
        wvo = sb("wvo", [C, C])
        small_s = sb("small_s", [C, 2 + 2 * E])
        gate_hl = sb("gate_hl", [C, 2, E], F16)
        w13_h = sb("w13_h", [C, E * 2 * HID], F16)
        w13_l = sb("w13_l", [C, E * 2 * HID], F16)
        w2_s = sb("w2_s", [C, E * HC * C])
        sw13_h = sb("sw13_h", [C, 2 * HID], F16)
        sw13_l = sb("sw13_l", [C, 2 * HID], F16)
        sw2_s = sb("sw2_s", [C, HC, C])
        tok_ident_s = sb("tok_ident_s", [C, 3, C])
        ident_h = sb("ident_h", [C, C], F16)
        powers = sb("powers", [C, BITS + 1])
        decay_rev = sb("decay_rev", [C, C])
        decay_len = sb("decay_len", [C, 1])
        masks_s = sb("masks_s", [L, 2 * L + 1])
        factor = sb("factor", [L, L + 1])
        mask = sb("mask", [L, L + 1])
        half_neg = sb("half_neg", [L, TILES])
        before_s = sb("before_s", [L, L], BF16)
        ones_s = sb("ones_s", [L, P], BF16)
        route_s = sb("route_s", [L, 2 * TILES * TOP + E + B])
        tiles_s = sb("tiles_s", [1, E + 2 * TABLE + 2 * ENDS])

        resid = sb("resid", [C, B, TILES * C])
        x_in = [sb(f"x_in{u}", [C, CHUNKS]) for u in range(2)]
        xn = [sb(f"xn{u}", [L, TILES, C]) for u in range(2)]
        xn_dec = [sb(f"xn_dec{u}", [L, TILES, C]) for u in range(2)]
        xn_t = [sb(f"xn_t{u}", [C, PTOK]) for u in range(2)]
        q_t = [sb(f"q_t{u}", [C, PTOK]) for u in range(2)]
        q_dec = [sb(f"q_dec{u}", [C, PTOK]) for u in range(2)]
        prob = [sb(f"prob{u}", [L, PTOK]) for u in range(2)]
        state = [sb(f"state{u}", [C, TILES, C]) for u in range(2)]
        ret_t = sb("ret_t", [C, PTOK])
        xn2 = [sb(f"xn2{u}", [L, TILES, C]) for u in range(2)]
        xn2_t = sb("xn2_t", [C, 2, 2, HTOK], F16)
        stats1 = sb("stats1", [L, TILES, 6])
        stats2 = sb("stats2", [L, TILES, 6])
        mv1 = sb("mv1", [L, TILES, 2])
        mv2 = sb("mv2", [L, TILES, 2])
        ve1 = sb("ve1", [L, TILES])
        ve2 = sb("ve2", [L, TILES])
        rstd1 = sb("rstd1", [L, TILES])
        neg_mean = sb("neg_mean", [L, TILES])
        shift1 = sb("shift1", [L, TILES])
        rstd2 = sb("rstd2", [L, TILES])
        raw = sb("raw", [L, TILES, E])
        biased = sb("biased", [L, TILES, E])
        top_raw = sb("top_raw", [L, TILES, 8])
        top_biased = sb("top_biased", [L, TILES, 8])
        top_idx = sb("top_idx", [L, TILES, 8], U32)
        idx_f = sb("idx_f", [L, TILES * TOP])
        iota_e = sb("iota_e", [L, E])
        chosen = sb("chosen", [L, TILES, TOP, E], BF16)
        assigned = sb("assigned", [L, TILES, E], BF16)
        assigned_sum = sb("assigned_sum", [L, E])
        taken = sb("taken", [L, E], BF16)
        taken_early = sb("taken_early", [L, E], BF16)
        place = sb("place", [L, TILES, E])
        chosen_place = sb("chosen_place", [L, TILES * TOP, E])
        place_sum = sb("place_sum", [L, TILES * TOP])
        dst = [sb(f"dst{u}", [L, TILES * TOP], I32) for u in range(2)]
        rows = [sb(f"rows{u}", [L, TOP, TILES, ROW]) for u in range(2)]
        top_val = sb("top_val", [L, TILES * TOP])
        top_sig = sb("top_sig", [L, TILES * TOP])
        share_sum = sb("share_sum", [L, TILES])
        filler = sb("filler", [P, SUB, ROW])
        fill_row = sb("fill_row", [1, E], I32)
        row_weight = sb("row_weight", [1, ENDS])
        count_i = sb("count_i", [1, 2, E], I32)
        tiles_i = sb("tiles_i", [1, 2, E], I32)
        tiles_f = sb("tiles_f", [1, ENDS + 1])
        tiles_all = sb("tiles_all", [1, E])
        region_move = sb("region_move", [1, E + 1])
        ones_e = sb("ones_e", [1, ENDS])
        tiles_end = sb("tiles_end", [1, ENDS])
        gated = sb("gated", [C, HTOK])
        hid = [sb(f"hid{u}", [C, HC, HTOK]) for u in range(2)]

        w_tok_s, ident_s = tok_ident_s[:, 0:2, :], tok_ident_s[:, 2, :]
        scal, gate_s, bias_s = small_s[:, 0:2], small_s[:, 2:2 + E], small_s[:, 2 + E:2 + 2 * E]
        causal_s, before_f = masks_s[:, 0:L + 1], masks_s[:, L + 1:2 * L + 1]
        pad_idx_s, pad_dst_s = (route_s[:, n * TILES * TOP:(n + 1) * TILES * TOP] for n in range(2))
        region_s = route_s[:, 2 * TILES * TOP:2 * TILES * TOP + E]
        early_s = route_s[:, 2 * TILES * TOP + E:2 * TILES * TOP + E + B]
        fill_base_s = tiles_s[:, 0:E]
        tile_no_s = tiles_s[:, E:E + 2 * TABLE].rearrange("p (n t) -> p n t", n=2)
        region_step_s, expert_step_s = (tiles_s[:, E + 2 * TABLE + n * ENDS:E + 2 * TABLE + (n + 1) * ENDS] for n in range(2))

        coef = hid[0][:].rearrange("p a b -> p (a b)")[:, 0:5 * C].rearrange("p (n c) -> p n c", n=5)
        proj_t = hid[1][:].rearrange("p a b -> p (a b)")[:, 0:4 * C].rearrange("p (n c) -> p n c", n=4)
        bits_s = q_dec[0][0:L, 0:BITS * (L + 1)].rearrange("p (n c) -> p n c", n=BITS)
        xg = [(x_in[0], x_in[1], ret_t)[n // 3][:, n % 3 * SUB * ROW:(n % 3 + 1) * SUB * ROW].rearrange("p (j w) -> p j w", w=ROW)
              for n in range(RING)]
        y_s = [state[0][:, n * SUB:(n + 1) * SUB, :] for n in range(YS)]
        xg_t = [q_t[0][:, n * R:(n + 1) * R].bitcast(F16).rearrange("p (h r) -> p h r", h=2) for n in range(2)]
        gate_e = [buf[:, 0:HC * R] for buf in (q_t[1], q_dec[0])]
        hid_e = [buf[:, 0:HC * R].rearrange("p (c r) -> p c r", c=HC) for buf in (q_dec[1], xn_t[0])]
        high = [rows[u][:, 0, :, 0:C // 2].bitcast(F16) for u in range(2)]
        low = [rows[u][:, 0, :, C // 2:C].bitcast(F16) for u in range(2)]
        stage_w13 = resid[:, B - 4:B, :].rearrange("p b n -> p (b n)")
        stage_sw13 = resid[:, B - 5, 0:2 * HID]
        ranges = ((0, LEAD + ONLY_EARLY, E), (LEAD + ONLY_EARLY, TABLE, ENDS))
        slot_past, slot_sum = ([buf[0:1].rearrange("p a b -> p (a b)")[:, 0:(b - a) * n].rearrange("p (t e) -> p t e", e=n)
                                for buf, (a, b, n) in zip(bufs, ranges)] for bufs in (xn, xn_dec))
        slot_expert, slot_start = (prob[0][0:1, n * TABLE:(n + 1) * TABLE] for n in range(2))
        slot_row, slot_w = (prob[1][0:1, n * TABLE:(n + 1) * TABLE].bitcast(I32) for n in range(2))
        y_back = [[xn[0], xn[1]], [xn_dec[0], xn_dec[1]], [xn2[0], xn2[1]], [state[0], state[1]]]

        ps = [ctx.enter_context(nc.psum_tensor(f"bank{i}", [C, 512], F32)) for i in range(8)]
        P_H, P_TR, P_QR, P_G, P_O, P_A1, P_A3, P_S = ps
        P_T, P_E1, P_E3, P_Y = (ps[0], ps[5]), (ps[1], ps[2]), (ps[3], ps[6]), (ps[4], ps[7])
        P_TR16 = P_TR[:].bitcast(F16)

        w_loaded, late_loaded = sem("w_loaded"), sem("late_loaded")
        proj_psum, proj_saved = sem("proj_psum"), sem("proj_saved")
        fold_psum, fold_saved = sem("fold_psum"), sem("fold_saved")
        dsig_ready, pw_step, mask_step, consts_ready = sem("dsig_ready"), sem("pw_step"), sem("mask_step"), sem("consts_ready")
        passed_dve, passed_pool, passed_pe = sem("passed_dve"), sem("passed_pool"), sem("passed_pe")
        passed_act = sem("passed_act")
        half_set, iota_set = sem("half_set"), sem("iota_set")
        x_loaded = [sem(f"x_loaded{u}") for u in range(2)]
        h_psum, h_saved = sem("h_psum"), sem("h_saved")
        stat_done, mean_done, ve1_done, rstd1_ready = sem("stat_done"), sem("mean_done"), sem("ve1_done"), sem("rstd1_ready")
        shift1_ready = sem("shift1_ready")
        xn_ready, xn_dec_ready = sem("xn_ready"), sem("xn_dec_ready")
        xn_t_psum, xn_t_ready = sem("xn_t_psum"), sem("xn_t_ready")
        q_psum, q_ready, q_dec_ready = sem("q_psum"), sem("q_ready"), sem("q_dec_ready")
        g_psum, state_step = sem("g_psum"), sem("state_step")
        s_psum, prob_ready = sem("s_psum"), sem("prob_ready")
        r_psum, ret_ready = sem("r_psum"), sem("ret_ready")
        o_psum, h2_ready = sem("o_psum"), sem("h2_ready")
        stat2_done, mean2_done, ve2_done, rstd2_ready = sem("stat2_done"), sem("mean2_done"), sem("ve2_done"), sem("rstd2_ready")
        xn2_ready = sem("xn2_ready")
        xn2_t_psum, xn2_t_ready = sem("xn2_t_psum"), sem("xn2_t_ready")
        gate_psum, gate_saved = sem("gate_psum"), sem("gate_saved")
        route_step, idx_ready, place_step = sem("route_step"), sem("idx_ready"), sem("place_step")
        a1_psum, a3_psum, gated_ready, hid_ready = sem("a1_psum"), sem("a3_psum"), sem("gated_ready"), sem("hid_ready")
        y_psum, y_added = sem("y_psum"), sem("y_added")
        xn2_copied, ids_ready = sem("xn2_copied"), sem("ids_ready")
        chosen_ready, place_psum, place_read, dst_ready = sem("chosen_ready"), sem("place_psum"), sem("place_read"), sem("dst_ready")
        rows_zeroed, filler_ready = sem("rows_zeroed"), sem("filler_ready")
        rows_sent = [sem(f"rows_sent{u}") for u in range(2)]
        filler_sent, count_psum, table_step, table_ready, fill_row_ready = sem("filler_sent"), sem("count_psum"), sem("table_step"), sem("table_ready"), sem("fill_row_ready")
        share_sig, share_step, share_ready = sem("share_sig"), sem("share_step"), sem("share_ready")
        weights_high, weights_split, ident_ready = sem("weights_high"), sem("weights_split"), sem("ident_ready")
        high_ready, low_ready = sem("high_ready"), sem("low_ready")
        xg_loaded = [sem(f"xg_loaded{n}") for n in range(RING)]
        y_sent = [sem(f"y_sent{n}") for n in range(RING)]
        xg_t_psum, xg_t_ready, e1_psum, e3_psum, gate_e_ready = sem("xg_t_psum"), sem("xg_t_ready"), sem("e1_psum"), sem("e3_psum"), sem("gate_e_ready")
        hid_e_ready, ye_psum, ye_saved = sem("hid_e_ready"), sem("ye_psum"), sem("ye_saved")
        y_loaded = [sem(f"y_loaded{u}") for u in range(BACK)]
        first_added, both_added = sem("first_added"), sem("both_added")
        out_stored = sem("out_stored")

        HALVES = (1, 0)
        SPLITS = 5
        LOADS = 5
        LATE_LOADS = 6
        block = ctx.enter_context(nc.Block())

        def stages(it, pair, u):
            def stage(lag):
                n = it - lag
                if isinstance(n, int) and not 0 <= n < B:
                    return None
                return n, (u - lag) % 2, pair + (u - lag) // 2
            return [stage(lag) for lag in range(5)]

        def last_batch(b):
            return isinstance(b, int) and b >= B - 2

        def steps(eng, step):
            for it in range(6):
                step(it, it // 2, it % 2)
            with eng.Fori(0, (B - 6) // 2) as i:
                for u in range(2):
                    step(i * 2 + (6 + u), i + 3, u)
            for it in range(B, B + 4):
                step(it, it // 2, it % 2)

        def slots(it, turn, n):
            def slot(lag):
                t = it - lag
                if isinstance(t, int) and not 0 <= t < SLOTS:
                    return None
                return t, (n - lag) % RING, turn + (n - lag) // RING
            return [slot(lag) for lag in range(3)]

        def slot_steps(eng, step, add_early=None):
            for it in range(RING):
                step(it, 0, it)
            with eng.Fori(1, BACK_TURN) as i:
                for n in range(RING):
                    step(i * RING + n, i, n)
            for n in range(RING):
                step(BACK_TURN * RING + n, BACK_TURN, n)
                if add_early:
                    add_early(0, 0, n)
            with eng.Fori(1, TURNS - BACK_TURN) as i:
                for n in range(RING):
                    step(i * RING + (BACK_TURN * RING + n), i + BACK_TURN, n)
                    if add_early:
                        add_early(i * 2, i, n)
            for it in range(TURNS * RING, SLOTS + 2):
                step(it, it // RING, it % RING)

        def table_entries(engine, table, at, count, most):
            return nc.values_load_multi_w_load_instructions(
                table[0:1, bass.ds(at, count)], engines=[engine], min_val=0, max_val=most,
                skip_runtime_bounds_check_because="the tables are sums of clamped counts, which stay in the range")[1]

        def store(eng, b):
            eng.wait_ge(both_added, b + 1)
            eng.dma_start(out[b, 0:(TILES - 1) * L, :].rearrange("(j p) d -> p j d", p=L),
                          resid[0:L, b, 0:(TILES - 1) * C].rearrange("p (j d) -> p j d", d=C)).then_inc(out_stored, 16)
            eng.dma_start(out[b, (TILES - 1) * L:FRAMES, :],
                          resid[0:REST, b, (TILES - 1) * C:TILES * C]).then_inc(out_stored, 16)

        @block.sync
        def _(sp):
            for to, src in ((small_s[:], small), (bits_s, exp_bits), (masks_s[:], masks)):
                sp.dma_start(to, src).then_inc(w_loaded, 16)

            def step(it, pair, u):
                s1 = stages(it, pair, u)[0]
                if s1:
                    b = s1[0]
                    if positive(2 * b - 2):
                        sp.wait_ge(h_psum, 2 * b - 2)
                    sp.dma_start(x_in[u][:], x_t[:, b, :]).then_inc(x_loaded[u], 16)
            steps(sp, step)

            sp.wait_ge(filler_ready, 1)
            for n in range(SPARE):
                sp.dma_start(routed[E * CAP + n * R:E * CAP + (n + 1) * R, :].rearrange("(j p) w -> p j w", p=P),
                             filler[:]).then_inc(filler_sent, 16)
            sp.wait_ge(fill_row_ready, 1)
            for e in range(0, E, 4):
                for row in table_entries(mybir.EngineType.SP, fill_row, e, 4, ROWS - R):
                    sp.dma_start(routed[bass.ds(row, R), :].rearrange("(j p) w -> p j w", p=P),
                                 filler[:]).then_inc(filler_sent, 16)
            for u in range(2):
                sp.wait_ge(rows_sent[u], 16 * TOP * TILES * B // 2)
            sp.wait_ge(filler_sent, 16 * (SPARE + E))
            sp.wait_ge(table_ready, 1)

            at_row = []

            def slot_step(it, turn, n):
                s1 = slots(it, turn, n)[0]
                if s1:
                    t, v, used = s1
                    if isinstance(t, int) and t == RING - 1:
                        sp.wait_ge(table_ready, 2)
                    if n % 4 == 0:
                        at_row[:] = table_entries(mybir.EngineType.SP, slot_row, t + LEAD, 4, ROWS - R)
                    row = at_row[n % 4]
                    if positive(used):
                        sp.wait_ge(y_sent[v], 16 * SUB * used)
                    sp.dma_start(xg[v], routed[bass.ds(row, R), :].rearrange("(j p) w -> p j w", p=P)).then_inc(xg_loaded[v], 16)
            full = (TILES - 1) * L

            def load_back(b, u, wait):
                if positive(wait):
                    sp.wait_ge(both_added, wait)
                for k in range(TOP):
                    at = b * (TOP * PTOK) + k * PTOK
                    sp.dma_start(y_back[u][k][0:L, 0:TILES - 1, :],
                                 results[bass.ds(at, full), :].rearrange("(j p) d -> p j d", p=L)).then_inc(y_loaded[u], 16)
                    sp.dma_start(y_back[u][k][0:REST, TILES - 1, :],
                                 results[bass.ds(at + full, REST), :]).then_inc(y_loaded[u], 16)

            def add_early(b, turn, n):
                if n in (1, 5):
                    u = n // 4
                    if isinstance(b, int):
                        load_back(u, u, 0)
                    else:
                        load_back(b + u, u, b + (u - 1))
                if n in (3, 7) and not isinstance(b, int):
                    store(sp, b + (n // 4 - 2))
            slot_steps(sp, slot_step, add_early)

            for b in range(ADDED, EARLY):
                load_back(b, b % BACK, b - 1)
            for n in range(RING):
                sp.wait_ge(y_sent[n], 16 * SUB * ((SLOTS - n + RING - 1) // RING))
            for b in range(EARLY, B):
                load_back(b, b % BACK, b + 1 - BACK if b >= EARLY + 2 else 0)

        @block.gpsimd
        def _(pool):
            nc.gpsimd.memset(half_neg[:], -0.5).then_inc(half_set, 1)
            nc.gpsimd.iota(iota_e[:], [[1, E]], base=0, channel_multiplier=0,
                           allow_small_or_imprecise_dtypes=True).then_inc(iota_set, 1)
            nc.gpsimd.memset(ones_s[:], 1.0).then_inc(iota_set, 1)
            nc.gpsimd.memset(ones_e[:], 1.0).then_inc(iota_set, 1)
            nc.gpsimd.memset(taken[:], 0.0).then_inc(iota_set, 1)
            nc.gpsimd.memset(taken_early[:], 0.0).then_inc(iota_set, 1)
            nc.gpsimd.memset(filler[:], 0.0).then_inc(rows_zeroed, 1)
            for u in range(2):
                nc.gpsimd.memset(rows[u][:], 0.0).then_inc(rows_zeroed, 1)
            pool.wait_ge(rows_zeroed, 3)
            nc.gpsimd.iota(filler[:, :, C:C + 1].rearrange("p j o -> p (j o)").bitcast(I32), [[0, SUB]], base=NOWHERE, channel_multiplier=0).then_inc(filler_ready, 1)
            for u in range(2):
                nc.gpsimd.iota(rows[u][:, :, :, C:C + 1].rearrange("p k j o -> p k (j o)").bitcast(I32),
                               [[PTOK, TOP], [L, TILES]], base=(u - 2) * TOP * PTOK, channel_multiplier=1).then_inc(filler_ready, 1)
            pool.wait_ge(half_set, 1)
            pool.wait_ge(consts_ready, 1)

            def step(it, pair, u):
                s1, _, s3, _, s5 = stages(it, pair, u)

                def send_rows(b, v, used, slices):
                    for n in slices:
                        j, k = n // TOP, n % TOP
                        nc.gpsimd.indirect_dma_start(routed, bass.IndirectOffsetOnAxis(dst[v][:, n:n + 1], 0),
                                                     rows[v][:, k, j, :], None, bounds_check=ROWS - 1,
                                                     oob_is_err=False).then_inc(rows_sent[v], 16)
                if s5:
                    b = s5[0]
                    pool.wait_ge(dst_ready, b + 1)
                    pool.wait_ge(xn2_copied, b + 1)
                    pool.wait_ge(ids_ready, b + 1)
                    pool.wait_ge(low_ready, b + 1)
                    pool.wait_ge(share_ready, b + 1)
                    pool.sem_inc(passed_pool, 1)
                    send_rows(*s5, range(12))
                if s3:
                    b = s3[0]
                    pool.wait_ge(mean2_done, b + 1)
                    pool.sem_inc(passed_pool, 1)
                    nc.gpsimd.tensor_scalar(ve2[:], mv2[:, :, 1], EPS, None, ALU.add).then_inc(ve2_done, 1)
                    pool.wait_ge(ve2_done, b + 1)
                    nc.gpsimd.tensor_tensor(rstd2[:], ve2[:], half_neg[:], ALU.pow).then_inc(rstd2_ready, 1)
                if s5:
                    send_rows(*s5, range(12, 14))
                if s1:
                    b = s1[0]
                    pool.wait_ge(mean_done, b + 1)
                    pool.sem_inc(passed_pool, 1)
                    nc.gpsimd.tensor_scalar(neg_mean[:], mv1[:, :, 0], -1.0, None, ALU.mult).then_inc(ve1_done, 1)
                    nc.gpsimd.tensor_scalar(ve1[:], mv1[:, :, 1], EPS, None, ALU.add).then_inc(ve1_done, 1)
                    if positive(b):
                        pool.wait_ge(xn_ready, b)
                    pool.wait_ge(ve1_done, 2 * b + 2)
                    nc.gpsimd.tensor_tensor(rstd1[:], ve1[:], half_neg[:], ALU.pow).then_inc(rstd1_ready, 1)
                    pool.wait_ge(rstd1_ready, b + 1)
                    nc.gpsimd.tensor_tensor(shift1[:], neg_mean[:], rstd1[:], ALU.mult).then_inc(shift1_ready, 1)
                if s5:
                    send_rows(*s5, range(14, TOP * TILES))
            steps(pool, step)

            def slot_step(it, turn, n):
                s3 = slots(it, turn, n)[2]
                if s3:
                    t, v, used = s3
                    pool.wait_ge(ye_saved, t + 1)
                    pool.sem_inc(passed_pool, 1)
                    for j in range(SUB):
                        nc.gpsimd.indirect_dma_start(results, bass.IndirectOffsetOnAxis(xg[v][:, j, C:C + 1].bitcast(I32), 0),
                                                     y_s[v % YS][:, j, :], None, bounds_check=RESULTS - 1,
                                                     oob_is_err=False).then_inc(y_sent[v], 16)
            slot_steps(pool, slot_step)

        @block.scalar
        def _(act):
            for to, src in ((coef, coefs_t), (tok_ident_s[:], tok_ident)):
                act.dma_start(to, src).then_inc(w_loaded, 16)
            for to, src in ((route_s[:], route), (tiles_s[:], tiles), (stage_sw13, sw13), (sw2_s[:], sw2)):
                act.dma_start(to, src).then_inc(late_loaded, 16)
            act.wait_ge(w_loaded, 16 * LOADS)
            for to, src in ((stage_w13, w13), (w2_s[:], w2)):
                act.dma_start(to, src).then_inc(late_loaded, 16)
            nc.scalar.activation(powers[:, 0:1], scal[:, 0:1], ACT.Sigmoid).then_inc(dsig_ready, 1)
            act.wait_ge(proj_psum, 1)
            nc.scalar.copy(ident_h[:], ident_s).then_inc(ident_ready, 1)
            nc.scalar.copy(proj_t, P_H[:].rearrange("p (n c) -> p n c", n=4)).then_inc(proj_saved, 1)
            act.wait_ge(fold_psum, 1)
            nc.scalar.copy(wqk[:], P_TR[:, 0:C]).then_inc(fold_saved, 1)
            nc.scalar.activation(wvo[:], P_TR[:, C:2 * C], ACT.Copy, scale=scal[:, 1:2]).then_inc(fold_saved, 1)

            def high_weights(n):
                if n == 0:
                    act.wait_ge(late_loaded, 16 * LATE_LOADS)
                    nc.scalar.copy(gate_hl[:, 0, :], gate_s).then_inc(weights_high, 1)
                    nc.scalar.copy(sw13_h[:], stage_sw13).then_inc(weights_high, 1)
                else:
                    part = slice((n - 1) * TILES * C, n * TILES * C)
                    nc.scalar.copy(w13_h[:, part], stage_w13[:, part]).then_inc(weights_high, 1)

            def step(it, pair, u):
                s1, s2, s3, s4, _ = stages(it, pair, u)

                def save_h(b, o):
                    if isinstance(b, int) and b == 5:
                        act.wait_ge(weights_split, SPLITS)
                    act.wait_ge(h_psum, 2 * b + o + 1)
                    nc.scalar.copy(resid[0:L, b, o * 512:(o + 1) * 512], P_H[0:L, :]).then_inc(h_saved, 1)

                def save_xn_t(b, v, used, o):
                    hf = HALVES[o]
                    act.wait_ge(xn_t_psum, 2 * b + o + 1)
                    if positive(2 * b - 2):
                        act.wait_ge(s_psum, 2 * b - 2)
                    nc.scalar.copy(xn_t[v][:, hf * HTOK:(hf + 1) * HTOK], P_S[:, 0:HTOK]).then_inc(xn_t_ready, 1)

                def save_ret(b, o):
                    hf = HALVES[o]
                    act.wait_ge(r_psum, 2 * b + o + 1)
                    if positive(2 * b):
                        act.wait_ge(o_psum, 2 * b)
                    nc.scalar.copy(ret_t[:, hf * HTOK:(hf + 1) * HTOK], P_QR[:, 0:HTOK]).then_inc(ret_ready, 1)

                def save_q(b, v, used, o):
                    hf = HALVES[o]
                    act.wait_ge(q_psum, 2 * b + o + 1)
                    if positive(2 * b - 2):
                        act.wait_ge(q_dec_ready, 2 * b - 2)
                    nc.scalar.copy(q_t[v][:, hf * HTOK:(hf + 1) * HTOK], P_QR[:, 0:HTOK]).then_inc(q_ready, 1)

                def save_xn2_t(b, z, used, o):
                    hf = HALVES[o]
                    act.wait_ge(xn2_t_psum, 2 * b + o + 1)
                    if positive(b):
                        act.wait_ge(a3_psum, 2 * HC * b)
                        act.wait_ge(gate_psum, b)
                    nc.scalar.copy(xn2_t[:, hf], P_TR16[:, 0:2 * HTOK].rearrange("p (h t) -> p h t", h=2)).then_inc(xn2_t_ready, 1)

                def gates(b, n):
                    act.wait_ge(a1_psum, 2 * HC * b + n + 1)
                    if positive(2 * HC * b + n):
                        act.wait_ge(hid_ready, 2 * HC * b + n)
                    nc.scalar.activation(gated[:], P_A1[:, 0:HTOK], ACT.Silu).then_inc(gated_ready, 1)

                def high_half(b, z, used):
                    act.wait_ge(xn2_ready, b + 1)
                    if positive(used):
                        act.wait_ge(rows_sent[z], 16 * TOP * TILES * used)
                    nc.scalar.copy(high[z], xn2[z][:]).then_inc(high_ready, 1)

                def second_rows(b, z, used):
                    act.wait_ge(low_ready, b + 1)
                    nc.scalar.copy(rows[z][:, 1, :, 0:C].bitcast(F16), rows[z][:, 0, :, 0:C].bitcast(F16)).then_inc(xn2_copied, 1)

                def norm1(b, v, used):
                    act.wait_ge(shift1_ready, b + 1)
                    if positive(2 * b - 2):
                        act.wait_ge(r_psum, 2 * b - 2)
                    act.sem_inc(passed_act, 1)
                    for t in range(TILES):
                        last = nc.scalar.activation(xn[v][:, t, :], resid[0:L, b, t * C:(t + 1) * C], ACT.Identity,
                                                    scale=rstd1[:, t:t + 1], bias=shift1[:, t:t + 1])
                    last.then_inc(xn_ready, 1)

                def decay_keys(b, v, used):
                    act.wait_ge(xn_ready, b + 1)
                    if positive(2 * b - 2):
                        act.wait_ge(g_psum, 2 * b - 2)
                    nc.scalar.activation(xn_dec[v][:], xn[v][:], ACT.Copy, scale=mask[:, 0:1]).then_inc(xn_dec_ready, 1)

                def sigmoids(b):
                    act.wait_ge(route_step, 4 * b + 4)
                    if positive(b):
                        act.wait_ge(share_ready, b)
                    nc.scalar.activation(top_sig[:], top_val[:], ACT.Sigmoid).then_inc(share_sig, 1)

                if s3:
                    save_ret(s3[0], 0)
                if s2:
                    save_xn_t(*s2, 0)
                if s1:
                    save_h(s1[0], 0)
                if s4:
                    save_xn2_t(*s4, 0)
                if s3:
                    save_ret(s3[0], 1)
                if s2:
                    save_xn_t(*s2, 1)
                if s4:
                    save_xn2_t(*s4, 1)
                    gates(s4[0], 0)
                if s2:
                    save_q(*s2, 0)
                    decay_keys(*s2)
                if s4 and last_batch(s4[0]):
                    second_rows(*s4)
                    sigmoids(s4[0])
                if s4:
                    gates(s4[0], 1)
                if s1:
                    save_h(s1[0], 1)
                if s2:
                    save_q(*s2, 1)
                if s4:
                    gates(s4[0], 2)
                if s4 and not last_batch(s4[0]):
                    second_rows(*s4)
                if s4:
                    gates(s4[0], 3)
                if isinstance(it, int) and 1 <= it < SPLITS:
                    if it == 1:
                        high_weights(0)
                    high_weights(it)
                if s4 and not last_batch(s4[0]):
                    sigmoids(s4[0])
                if s1:
                    norm1(*s1)
                if s3:
                    high_half(*s3)
            steps(act, step)

            def slot_step(it, turn, n):
                s1, s2, _ = slots(it, turn, n)
                if s1:
                    t, v, used = s1
                    act.wait_ge(xg_t_psum, t + 1)
                    if positive(t - 1):
                        act.wait_ge(e3_psum, t - 1)
                    nc.scalar.copy(xg_t[v % 2], P_T[v % 2][:].bitcast(F16)[:, 0:2 * R].rearrange("p (h r) -> p h r", h=2)).then_inc(xg_t_ready, 1)
                if s2:
                    t, v, used = s2
                    act.wait_ge(e1_psum, t + 1)
                    if positive(t - 1):
                        act.wait_ge(hid_e_ready, t - 1)
                    nc.scalar.activation(gate_e[v % 2], P_E1[v % 2][:], ACT.Silu).then_inc(gate_e_ready, 1)
            slot_steps(act, slot_step)

            with act.Fori(ADDED - 2, B) as b:
                store(act, b)
            act.wait_ge(out_stored, 32 * B)

        @block.vector
        def _(dve):
            dve.wait_ge(dsig_ready, 1)
            nstep = 0
            for n in range(BITS - 1):
                nc.vector.tensor_tensor(powers[:, n + 1:n + 2], powers[:, n:n + 1], powers[:, n:n + 1], ALU.mult).then_inc(pw_step, 1)
                nstep += 1
                dve.wait_ge(pw_step, nstep)
            nc.vector.memset(decay_rev[:, C - 1:C], 1.0).then_inc(pw_step, 1)
            nstep += 1
            for n in range(BITS):
                dve.wait_ge(pw_step, nstep)
                w = 2 ** n
                nc.vector.tensor_scalar(decay_rev[:, C - 2 * w:C - w], decay_rev[:, C - w:C], powers[:, n:n + 1], None, ALU.mult).then_inc(pw_step, 1)
                nstep += 1
            dve.wait_ge(pw_step, nstep)
            nc.vector.tensor_copy(decay_len[:], decay_rev[:, C - 1 - L:C - L]).then_inc(pw_step, 1)
            nc.vector.tensor_copy(mask[:], causal_s).then_inc(mask_step, 1)
            m = 1
            for n in range(BITS):
                dve.wait_ge(mask_step, m)
                nc.vector.tensor_scalar(factor[:], bits_s[:, n, :], -1.0, 1.0, ALU.mult, ALU.add).then_inc(mask_step, 1)
                dve.wait_ge(mask_step, m + 1)
                nc.vector.scalar_tensor_tensor(out=factor[:], in0=bits_s[:, n, :], scalar=powers[0:L, n:n + 1],
                                               in1=factor[:], op0=ALU.mult, op1=ALU.max).then_inc(mask_step, 1)
                dve.wait_ge(mask_step, m + 2)
                last = nc.vector.tensor_tensor(mask[:], mask[:], factor[:], ALU.mult)
                last.then_inc(mask_step, 1)
                m += 3
            dve.wait_ge(mask_step, m)
            dve.wait_ge(pw_step, nstep + 1)
            nc.vector.tensor_scalar(factor[:, 0:1], mask[:, 0:1], 1.0, None, ALU.mult).then_inc(consts_ready, 1)
            dve.wait_ge(iota_set, 5)
            dve.wait_ge(filler_ready, 3)
            nc.vector.tensor_copy(before_s[:], before_f).then_inc(consts_ready, 1)

            def means(b, src, stats, done, aggregated, mv):
                dve.sem_inc(passed_dve, 1)
                for t in range(TILES):
                    last = nc.vector.bn_stats(stats[:, t, :], src[:, t * C:(t + 1) * C])
                last.then_inc(done, 1)
                dve.wait_ge(done, b + 1)
                dve.sem_inc(passed_dve, 1)
                for t in range(TILES):
                    last = nc.vector.bn_aggr(mv[:, t, :], stats[:, t, :])
                last.then_inc(aggregated, 1)

            def low_weights(n):
                dve.wait_ge(weights_high, n + 2)
                if n == 0:
                    nc.vector.tensor_tensor(gate_hl[:, 1, :], gate_s, gate_hl[:, 0, :], ALU.subtract)
                    nc.vector.tensor_tensor(sw13_l[:], stage_sw13, sw13_h[:], ALU.subtract).then_inc(weights_split, 1)
                else:
                    part = slice((n - 1) * TILES * C, n * TILES * C)
                    nc.vector.tensor_tensor(w13_l[:, part], stage_w13[:, part], w13_h[:, part], ALU.subtract).then_inc(weights_split, 1)

            def step(it, pair, u):
                s1, s2, s3, s4, s5 = stages(it, pair, u)

                def hidden(b, n):
                    o, hc = n // HC, n % HC
                    g = 2 * HC * b + n
                    dve.wait_ge(gated_ready, g + 1)
                    dve.wait_ge(a3_psum, g + 1)
                    if positive(2 * b + o - 1):
                        dve.wait_ge(y_psum, 2 * b + o - 1)
                    nc.vector.tensor_tensor(hid[o][:, hc, :], gated[:], P_A3[:, 0:HTOK], ALU.mult).then_inc(hid_ready, 1)

                def add_half(b, o, bank, made, added):
                    hf = HALVES[o]
                    dve.wait_ge(made, 2 * b + o + 1)
                    part = resid[0:L, b, hf * 512:(hf + 1) * 512]
                    nc.vector.tensor_tensor(part, bank[0:L, :], part, ALU.add).then_inc(added, 1)

                def decay_queries(b, v, o):
                    cols = slice(HALVES[o] * HTOK, (HALVES[o] + 1) * HTOK)
                    dve.wait_ge(q_ready, 2 * b + o + 1)
                    if positive(2 * b - 2):
                        dve.wait_ge(r_psum, 2 * b - 2)
                    nc.vector.tensor_tensor(q_dec[v][:, cols].rearrange("p (j t) -> p j t", t=L),
                                            q_t[v][:, cols].rearrange("p (j t) -> p j t", t=L),
                                            decay_rev[:, C - L:C].unsqueeze(1).to_broadcast([C, HT, L]),
                                            ALU.mult).then_inc(q_dec_ready, 1)

                def mask_scores(b, v, o):
                    cols = slice(HALVES[o] * HTOK, (HALVES[o] + 1) * HTOK)
                    dve.wait_ge(s_psum, 2 * b + o + 1)
                    nc.vector.tensor_tensor(prob[v][:, cols].rearrange("p (j t) -> p j t", t=L),
                                            P_S[0:L, 0:HTOK].rearrange("p (j t) -> p j t", t=L),
                                            mask[:, 1:L + 1].unsqueeze(1).to_broadcast([L, HT, L]),
                                            ALU.mult).then_inc(prob_ready, 1)

                def states(b, v, o):
                    dve.wait_ge(g_psum, 2 * b + o + 1)
                    for n, c in enumerate((3, 2, 1) if o else (7, 6, 5, 4)):
                        part = P_G[:, n * C:(n + 1) * C]
                        if c == TILES - 1:
                            nc.vector.tensor_copy(state[v][:, c - 1, :], part).then_inc(state_step, 1)
                        else:
                            dve.wait_ge(state_step, 7 * b + (7 - c))
                            nc.vector.scalar_tensor_tensor(out=state[v][:, c - 1, :], in0=state[v][:, c, :],
                                                           scalar=decay_len[:, 0:1], in1=part,
                                                           op0=ALU.mult, op1=ALU.add).then_inc(state_step, 1)

                def send_places(b, z, used):
                    dve.wait_ge(place_psum, b + 1)
                    nc.vector.tensor_tensor(place[:], P_O[0:L, 0:TILES * E].rearrange("p (j e) -> p j e", e=E),
                                            region_s.unsqueeze(1).to_broadcast([L, TILES, E]), ALU.add).then_inc(place_read, 1)
                    nc.vector.tensor_reduce(assigned_sum[:], assigned[:].rearrange("p j e -> p e j"), AX.X, ALU.add).then_inc(place_step, 1)
                    dve.wait_ge(place_step, 4 * b + 1)
                    dve.wait_ge(place_read, b + 1)
                    nc.vector.scalar_tensor_tensor(out=taken_early[:], in0=assigned_sum[:], scalar=early_s[:, bass.ds(b, 1)],
                                                   in1=taken_early[:], op0=ALU.mult, op1=ALU.add)
                    nc.vector.tensor_tensor(taken[:], taken[:], assigned_sum[:], ALU.add).then_inc(place_step, 1)
                    nc.vector.tensor_tensor(chosen_place[:].rearrange("p (j k) e -> p j k e", k=TOP), chosen[:],
                                            place[:].unsqueeze(2).to_broadcast([L, TILES, TOP, E]), ALU.mult).then_inc(place_step, 1)
                    dve.wait_ge(place_step, 4 * b + 3)
                    nc.vector.tensor_reduce(place_sum[:], chosen_place[:], AX.X, ALU.add).then_inc(place_step, 1)
                    if positive(used):
                        dve.wait_ge(rows_sent[z], 16 * TOP * TILES * used)
                    dve.wait_ge(place_step, 4 * b + 4)
                    nc.vector.tensor_tensor(dst[z][:], place_sum[:], pad_dst_s, ALU.add).then_inc(dst_ready, 1)
                    ids = rows[z][:, :, :, C:C + 1].rearrange("p k j o -> p k (j o)").bitcast(I32)
                    nc.vector.tensor_scalar(ids, ids, 2.0 * TOP * PTOK, None, ALU.add).then_inc(ids_ready, 1)
                    dve.wait_ge(share_sig, b + 1)
                    nc.vector.tensor_reduce(share_sum[:], top_sig[:].rearrange("p (j k) -> p j k", k=TOP), AX.X, ALU.add).then_inc(share_step, 1)
                    dve.wait_ge(share_step, 2 * b + 1)
                    nc.vector.reciprocal(share_sum[:], share_sum[:]).then_inc(share_step, 1)
                    dve.wait_ge(share_step, 2 * b + 2)
                    nc.vector.tensor_tensor(rows[z][:, :, :, C + 1:C + 2].rearrange("p k j o -> p k (j o)"),
                                            top_sig[:].rearrange("p (j k) -> p k j", k=TOP),
                                            share_sum[:].unsqueeze(1).to_broadcast([L, TOP, TILES]), ALU.mult).then_inc(share_ready, 1)

                def low_half(b, z, used):
                    dve.wait_ge(high_ready, b + 1)
                    nc.vector.tensor_tensor(low[z], xn2[z][:], high[z], ALU.subtract).then_inc(low_ready, 1)

                def read_scores(b):
                    if isinstance(b, int) and b == 0:
                        dve.wait_ge(late_loaded, 16 * LATE_LOADS)
                    dve.wait_ge(gate_psum, b + 1)
                    nc.vector.tensor_copy(raw[:].rearrange("p j e -> p (j e)"), P_G[0:L, 0:TILES * E]).then_inc(route_step, 1)
                    nc.vector.tensor_tensor(biased[:], P_G[0:L, 0:TILES * E].rearrange("p (j e) -> p j e", e=E),
                                            bias_s[0:L, :].unsqueeze(1).to_broadcast([L, TILES, E]), ALU.add).then_inc(gate_saved, 1)

                def best_scores(b):
                    dve.wait_ge(route_step, 4 * b + 1)
                    dve.wait_ge(gate_saved, b + 1)
                    dve.sem_inc(passed_dve, 1)
                    for t in range(TILES):
                        nc.vector.max(top_biased[:, t, :], biased[:, t, :])
                        last = nc.vector.max(top_raw[:, t, :], raw[:, t, :])
                    last.then_inc(route_step, 1)

                def choose(b):
                    dve.wait_ge(route_step, 4 * b + 2)
                    dve.sem_inc(passed_dve, 1)
                    for t in range(TILES):
                        last = nc.vector.max_index(top_idx[:, t, :], top_biased[:, t, :], biased[:, t, :])
                    last.then_inc(route_step, 1)
                    nc.vector.tensor_copy(top_val[:].rearrange("p (j k) -> p j k", k=TOP), top_raw[:, :, 0:TOP]).then_inc(route_step, 1)
                    dve.wait_ge(route_step, 4 * b + 4)
                    nc.vector.tensor_tensor(idx_f[:].rearrange("p (j k) -> p j k", k=TOP), top_idx[:, :, 0:TOP],
                                            pad_idx_s.rearrange("p (j k) -> p j k", k=TOP), ALU.add).then_inc(idx_ready, 1)
                    dve.wait_ge(idx_ready, b + 1)
                    nc.vector.tensor_tensor(chosen[:].rearrange("p j k e -> p (j k) e"),
                                            iota_e[:].unsqueeze(1).to_broadcast([L, TILES * TOP, E]),
                                            idx_f[:].unsqueeze(2).to_broadcast([L, TILES * TOP, E]), ALU.is_equal).then_inc(chosen_ready, 1)
                    dve.wait_ge(chosen_ready, 2 * b + 1)
                    nc.vector.tensor_tensor(assigned[:], chosen[:, :, 0, :], chosen[:, :, 1, :], ALU.add).then_inc(chosen_ready, 1)

                def means2(b):
                    dve.wait_ge(h2_ready, 2 * b + 2)
                    if positive(b):
                        dve.wait_ge(rstd2_ready, b)
                    means(b, resid[0:L, b, :], stats2, stat2_done, mean2_done, mv2)

                def means1(b):
                    dve.wait_ge(h_saved, 2 * b + 2)
                    if positive(b):
                        dve.wait_ge(rstd1_ready, b)
                    means(b, resid[0:L, b, :], stats1, stat_done, mean_done, mv1)

                def norm2(b, w, used):
                    dve.wait_ge(rstd2_ready, b + 1)
                    if positive(2 * b - 2):
                        dve.wait_ge(high_ready, b - 1)
                        dve.wait_ge(low_ready, b - 1)
                    for t in range(TILES):
                        last = nc.vector.tensor_scalar(xn2[w][:, t, :], resid[0:L, b, t * C:(t + 1) * C],
                                                       mv2[:, t, 0:1], rstd2[:, t:t + 1], ALU.subtract, ALU.mult)
                    last.then_inc(xn2_ready, 1)

                if s5:
                    add_half(s5[0], 1, P_H, y_psum, y_added)
                if s3:
                    states(s3[0], s3[1], 1)
                    decay_queries(s3[0], s3[1], 1)
                if s4:
                    low_half(*s4)
                if s5 and not last_batch(s5[0]):
                    send_places(*s5)
                if s4:
                    read_scores(s4[0])
                if s3:
                    add_half(s3[0], 0, P_O, o_psum, h2_ready)
                if s4:
                    best_scores(s4[0])
                    hidden(s4[0], 0)
                    choose(s4[0])
                if s3:
                    add_half(s3[0], 1, P_O, o_psum, h2_ready)
                    means2(s3[0])
                if s4 and last_batch(s4[0]):
                    send_places(*s4)
                if s4:
                    hidden(s4[0], 1)
                if s2:
                    decay_queries(s2[0], s2[1], 0)
                if s1:
                    means1(s1[0])
                if s2:
                    mask_scores(s2[0], s2[1], 0)
                    states(s2[0], s2[1], 0)
                if s4:
                    hidden(s4[0], 2)
                    add_half(s4[0], 0, P_H, y_psum, y_added)
                if s2:
                    mask_scores(s2[0], s2[1], 1)
                if s4:
                    hidden(s4[0], 3)
                if s3:
                    norm2(*s3)
                if isinstance(it, int) and 1 <= it < SPLITS:
                    if it == 1:
                        low_weights(0)
                    low_weights(it)
            steps(dve, step)

            dve.wait_ge(count_psum, 1)
            nc.vector.tensor_tensor(fill_row[:], P_O[0:1, 0:E], fill_base_s, ALU.add).then_inc(fill_row_ready, 1)
            nc.vector.memset(tiles_f[:], 0.0).then_inc(table_step, 1)
            nc.vector.tensor_scalar(count_i[:], P_O[0:1, 0:2 * E].rearrange("p (g e) -> p g e", g=2), R - 1.0, None, ALU.add).then_inc(table_step, 1)
            dve.wait_ge(table_step, 2)
            nc.vector.tensor_scalar(tiles_i[:], count_i[:], R.bit_length() - 1, None, ALU.logical_shift_right).then_inc(table_step, 1)
            dve.wait_ge(table_step, 3)
            nc.vector.tensor_copy(tiles_f[:, 1:E + 1], tiles_i[:, 1, :]).then_inc(table_step, 1)
            nc.vector.tensor_copy(tiles_all[:], tiles_i[:, 0, :]).then_inc(table_step, 1)
            dve.wait_ge(table_step, 5)
            nc.vector.tensor_tensor(tiles_f[:, E + 2:ENDS + 1], tiles_all[:], tiles_f[:, 1:E + 1], ALU.subtract).then_inc(table_step, 1)
            nc.vector.tensor_tensor(region_move[:], tiles_f[:, 1:E + 2], tiles_f[:, 0:E + 1], ALU.subtract).then_inc(table_step, 1)
            dve.wait_ge(table_step, 7)
            nc.vector.scalar_tensor_tensor(out=row_weight[:], in0=tiles_f[:, 1:ENDS + 1], scalar=-float(R), in1=region_step_s,
                                           op0=ALU.mult, op1=ALU.add).then_inc(table_step, 1)
            nc.vector.tensor_tensor_scan(tiles_end[:], ones_e[:], tiles_f[:, 1:ENDS + 1], 0.0, ALU.mult, ALU.add).then_inc(table_step, 1)
            dve.wait_ge(table_step, 8)
            nc.vector.scalar_tensor_tensor(out=row_weight[:, E:ENDS], in0=region_move[:], scalar=float(R), in1=row_weight[:, E:ENDS],
                                           op0=ALU.mult, op1=ALU.add).then_inc(table_step, 1)
            dve.wait_ge(xn_dec_ready, B)
            dve.wait_ge(r_psum, 2 * B)
            step_no = 10
            for g, (a, b, n) in enumerate(ranges):
                dve.wait_ge(table_step, step_no)
                nc.vector.tensor_tensor(slot_past[g], tiles_end[:, 0:n].unsqueeze(1).to_broadcast([1, b - a, n]),
                                        tile_no_s[:, 0, a:b].unsqueeze(2).to_broadcast([1, b - a, n]), ALU.is_le).then_inc(table_step, 1)
                dve.wait_ge(table_step, step_no + 1)
                nc.vector.tensor_tensor(slot_sum[g], slot_past[g], row_weight[:, 0:n].unsqueeze(1).to_broadcast([1, b - a, n]), ALU.mult).then_inc(table_step, 1)
                if g:
                    dve.wait_ge(table_step, step_no + 2)
                    nc.vector.tensor_tensor(slot_past[g], slot_past[g], expert_step_s.unsqueeze(1).to_broadcast([1, b - a, n]), ALU.mult).then_inc(table_step, 1)
                    step_no += 1
                    dve.wait_ge(table_step, step_no + 2)
                nc.vector.tensor_reduce(slot_expert[:, a:b], slot_past[g], AX.X, ALU.add).then_inc(table_step, 1)
                dve.wait_ge(table_step, step_no + 3)
                nc.vector.tensor_reduce(slot_start[:, a:b], slot_sum[g], AX.X, ALU.add).then_inc(table_step, 1)
                dve.wait_ge(table_step, step_no + 4)
                nc.vector.tensor_tensor(slot_row[:, a:b], tile_no_s[:, 1, a:b], slot_start[:, a:b], ALU.add)
                last = nc.vector.tensor_scalar(slot_w[:, a:b], slot_expert[:, a:b], E - 1.0, float(HC * C), ALU.min, ALU.mult)
                last.then_inc(table_step, 1)
                step_no += 5
                dve.wait_ge(table_step, step_no)
                dve.sem_inc(table_ready, 1)

            def slot_step(it, turn, n):
                _, s2, s3 = slots(it, turn, n)
                if s2:
                    t, v, used = s2
                    dve.wait_ge(gate_e_ready, t + 1)
                    dve.wait_ge(e3_psum, t + 1)
                    if positive(t - 1):
                        dve.wait_ge(ye_psum, t - 1)
                    nc.vector.tensor_tensor(hid_e[v % 2], gate_e[v % 2].rearrange("p (c r) -> p c r", c=HC),
                                            P_E3[v % 2][:].rearrange("p (c r) -> p c r", c=HC), ALU.mult).then_inc(hid_e_ready, 1)
                if s3:
                    t, v, used = s3
                    dve.wait_ge(ye_psum, t + 1)
                    if v >= YS:
                        dve.wait_ge(y_sent[v - YS], 16 * SUB * (used + 1))
                    elif positive(used):
                        dve.wait_ge(y_sent[v + RING - YS], 16 * SUB * used)
                    for j in range(SUB):
                        last = nc.vector.tensor_scalar(y_s[v % YS][:, j, :], P_Y[v % 2][:, j * C:(j + 1) * C],
                                                       xg[v][:, j, C + 1:C + 2], None, ALU.mult)
                    last.then_inc(ye_saved, 1)

            def add_back(b, u, used):
                dve.wait_ge(y_loaded[u], 64 * used + 64)
                for k in range(TOP):
                    if k:
                        dve.wait_ge(first_added, b + 1)
                    for rows_of, tiles in ((L, slice(0, TILES - 1)), (REST, slice(TILES - 1, TILES))):
                        part = resid[0:rows_of, b, tiles.start * C:tiles.stop * C].rearrange("p (j c) -> p j c", c=C)
                        last = nc.vector.tensor_tensor(part, y_back[u][k][0:rows_of, tiles, :], part, ALU.add)
                    last.then_inc(both_added if k else first_added, 1)

            def add_early(b, turn, n):
                if n in (3, 7):
                    u = n // 4
                    add_back(b + u, u, turn)
            slot_steps(dve, slot_step, add_early)
            for b in range(ADDED, B):
                add_back(b, b % BACK, (ADDED // 2 if b % BACK < 2 else 0) + (b - ADDED) // BACK)

        @block.tensor
        def _(pe):
            pe.wait_ge(w_loaded, 16 * LOADS)
            def split_product(to, w_high, w_low, x):
                nc.tensor.matmul(to, w_high, x[:, 0, :], start=True, stop=False)
                nc.tensor.matmul(to, w_high, x[:, 1, :], start=False, stop=False)
                return nc.tensor.matmul(to, w_low, x[:, 0, :], start=False, stop=True)

            for n in range(4):
                last = nc.tensor.matmul(P_H[:, n * C:(n + 1) * C], coef[:, n + 1, :], coef[:, 0, :], start=True, stop=True)
            last.then_inc(proj_psum, 1)
            pe.wait_ge(proj_saved, 1)
            nc.tensor.matmul(P_TR[:, 0:C], proj_t[:, 0, :], proj_t[:, 1, :], start=True, stop=True)
            nc.tensor.matmul(P_TR[:, C:2 * C], proj_t[:, 2, :], proj_t[:, 3, :], start=True, stop=True).then_inc(fold_psum, 1)
            pe.wait_ge(fold_saved, 2)

            def step(it, pair, u):
                s1, s2, s3, s4, _ = stages(it, pair, u)

                def tokens(b, o):
                    if o == 0:
                        pe.wait_ge(x_loaded[u], 16 * pair + 16)
                    if positive(2 * b - 6) and o == 0:
                        pe.wait_ge(y_added, 2 * b - 6)
                    if positive(2 * b + o):
                        pe.wait_ge(h_saved, 2 * b + o)
                    for j in range(HT):
                        m = (HT * o + j) * L
                        nc.tensor.matmul(P_H[0:L, j * C:(j + 1) * C], x_in[u][:, m:m + L], w_tok_s[:, 0, :], start=True, stop=False)
                        last = nc.tensor.matmul(P_H[0:L, j * C:(j + 1) * C], x_in[u][:, m + 1:m + 1 + L], w_tok_s[:, 1, :], start=False, stop=True)
                    last.then_inc(h_psum, 1)

                def turn(b, v, used, o):
                    if o == 0:
                        pe.wait_ge(xn_ready, b + 1)
                    if positive(2 * b + o):
                        pe.wait_ge(xn_t_ready, 2 * b + o)
                    if o == 0 and positive(2 * b):
                        pe.wait_ge(prob_ready, 2 * b)
                    for j in range(HT):
                        last = nc.tensor.transpose(P_S[:, j * L:(j + 1) * L], xn[v][:, HT * HALVES[o] + j, :], ident_s[0:L, 0:L])
                    last.then_inc(xn_t_psum, 1)

                def retrieve(b, w, used, o):
                    pe.wait_ge(prob_ready, 2 * b + o + 1)
                    pe.wait_ge(state_step, 7 * b + (7 if o else 4))
                    pe.wait_ge(q_dec_ready, 2 * b + o + 1)
                    if o == 0:
                        pe.wait_ge(q_ready, 2 * b + 2)
                    if positive(2 * b + o):
                        pe.wait_ge(ret_ready, 2 * b + o)
                    for j in range(HT):
                        c = HT * HALVES[o] + j
                        tok = slice(c * L, (c + 1) * L)
                        dst = P_QR[:, j * L:(j + 1) * L]
                        last = nc.tensor.matmul(dst, xn[w][:, c, :], prob[w][:, tok], start=True, stop=(c == TILES - 1))
                        if c < TILES - 1:
                            last = nc.tensor.matmul(dst, state[w][:, c, :], q_dec[w][:, tok], start=False, stop=True)
                    last.then_inc(r_psum, 1)

                def queries(b, v, used, o):
                    pe.wait_ge(xn_t_ready, 2 * b + o + 1)
                    if positive(2 * b + o):
                        pe.wait_ge(q_ready, 2 * b + o)
                    if positive(2 * b):
                        pe.wait_ge(ret_ready, 2 * b)
                    cols = slice(HALVES[o] * HTOK, (HALVES[o] + 1) * HTOK)
                    nc.tensor.matmul(P_QR[:, 0:HTOK], wqk[:], xn_t[v][:, cols], start=True, stop=True).then_inc(q_psum, 1)

                def project(b, o):
                    pe.wait_ge(ret_ready, 2 * b + o + 1)
                    if positive(2 * b + o):
                        pe.wait_ge(h2_ready, 2 * b + o)
                    if positive(b - 1):
                        pe.wait_ge(place_read, b - 1)
                    for j in range(HT):
                        c = HT * HALVES[o] + j
                        last = nc.tensor.matmul(P_O[0:L, j * C:(j + 1) * C], ret_t[:, c * L:(c + 1) * L], wvo[:], start=True, stop=True)
                    last.then_inc(o_psum, 1)

                def keys(b, v, used, o):
                    if o == 0:
                        pe.wait_ge(xn_dec_ready, b + 1)
                        if positive(b - 1):
                            pe.wait_ge(gate_saved, b - 1)
                    if positive(7 * b + 4 * o):
                        pe.wait_ge(state_step, 7 * b + 4 * o)
                    for n, c in enumerate((3, 2, 1) if o else (7, 6, 5, 4)):
                        last = nc.tensor.matmul(P_G[:, n * C:(n + 1) * C], xn_dec[v][:, c, :], xn[v][:, c, :], start=True, stop=True)
                    last.then_inc(g_psum, 1)

                def scores(b, v, used, o):
                    pe.wait_ge(q_ready, 2 * b + o + 1)
                    if positive(2 * b + o):
                        pe.wait_ge(prob_ready, 2 * b + o)
                    for j in range(HT):
                        c = HT * HALVES[o] + j
                        tok = slice(c * L, (c + 1) * L)
                        last = nc.tensor.matmul(P_S[0:L, j * L:(j + 1) * L], xn_t[v][:, tok], q_t[v][:, tok], start=True, stop=True)
                    last.then_inc(s_psum, 1)

                def turn2(b, z, used, o):
                    if o == 0:
                        if isinstance(b, int) and b == 0:
                            pe.wait_ge(ident_ready, 1)
                            pe.wait_ge(consts_ready, 2)
                            pe.wait_ge(iota_set, 5)
                            pe.wait_ge(weights_split, 1)
                        pe.wait_ge(low_ready, b + 1)
                    if positive(2 * b + o):
                        pe.wait_ge(xn2_t_ready, 2 * b + o)
                    for h, half in enumerate((high[z], low[z])):
                        for j in range(HT):
                            last = nc.tensor.transpose(P_TR16[:, h * HTOK + j * L:h * HTOK + (j + 1) * L],
                                                       half[:, HT * HALVES[o] + j, :], ident_h[0:L, 0:L])
                    last.then_inc(xn2_t_psum, 1)

                def gate(b):
                    pe.wait_ge(xn2_t_ready, 2 * b + 2)
                    pe.wait_ge(state_step, cap(7 * b + 14, 7 * B))
                    if positive(b):
                        pe.wait_ge(gate_saved, b)
                    for c in range(TILES):
                        for n, (h, g) in enumerate(((0, 0), (0, 1), (1, 0))):
                            last = nc.tensor.matmul(P_G[0:L, c * E:(c + 1) * E], xn2_t[:, c // HT, h, c % HT * L:(c % HT + 1) * L],
                                                    gate_hl[:, g, :], start=(n == 0), stop=(n == 2))
                    last.then_inc(gate_psum, 1)

                def expand(b, n):
                    o, hc = n // HC, n % HC
                    g = 2 * HC * b + n
                    if positive(g):
                        pe.wait_ge(gated_ready, g)
                    split_product(P_A1[:, 0:HTOK], sw13_h[:, hc * C:(hc + 1) * C], sw13_l[:, hc * C:(hc + 1) * C],
                                  xn2_t[:, HALVES[o]]).then_inc(a1_psum, 1)
                    if positive(g):
                        pe.wait_ge(hid_ready, g)
                    at = HID + hc * C
                    split_product(P_A3[:, 0:HTOK], sw13_h[:, at:at + C], sw13_l[:, at:at + C],
                                  xn2_t[:, HALVES[o]]).then_inc(a3_psum, 1)

                def contract(b, o):
                    pe.wait_ge(hid_ready, 2 * HC * b + HC * (o + 1))
                    pe.wait_ge(h_saved, cap(2 * b + 8, 2 * B))
                    if positive(2 * b + o):
                        pe.wait_ge(y_added, 2 * b + o)
                    for j in range(HT):
                        for hc in range(HC):
                            last = nc.tensor.matmul(P_H[0:L, j * C:(j + 1) * C], hid[o][:, hc, j * L:(j + 1) * L], sw2_s[:, hc, :],
                                                    start=(hc == 0), stop=(hc == HC - 1))
                    last.then_inc(y_psum, 1)

                def places(b):
                    pe.wait_ge(chosen_ready, 2 * b + 2)
                    pe.wait_ge(h2_ready, cap(2 * b + 4, 2 * B))
                    if positive(b):
                        pe.wait_ge(place_step, 4 * b)
                    nc.tensor.matmul(P_O[0:L, 0:TILES * E], before_s[:], assigned[:].rearrange("p j e -> p (j e)"), start=True, stop=False)
                    nc.tensor.matmul(P_O[0:L, 0:TILES * E], ones_s[:, 0:L], taken[:].unsqueeze(1).to_broadcast([L, TILES, E]), start=False, stop=False)
                    for j in range(TILES - 1):
                        last = nc.tensor.matmul(P_O[0:L, (j + 1) * E:TILES * E], ones_s[:, 0:L],
                                                assigned[:, j:j + 1, :].to_broadcast([L, TILES - 1 - j, E]),
                                                start=False, stop=(j == TILES - 2))
                    last.then_inc(place_psum, 1)

                if s3:
                    retrieve(*s3, 0)
                if s1:
                    tokens(s1[0], 0)
                if s2:
                    turn(*s2, 0)
                if s4:
                    turn2(*s4, 0)
                if s3:
                    retrieve(*s3, 1)
                if s2:
                    turn(*s2, 1)
                if s4:
                    turn2(*s4, 1)
                if s3:
                    project(s3[0], 0)
                if s4:
                    gate(s4[0])
                    expand(s4[0], 0)
                if s1:
                    tokens(s1[0], 1)
                if s3:
                    project(s3[0], 1)
                if s2:
                    queries(*s2, 0)
                if s4 and last_batch(s4[0]):
                    places(s4[0])
                if s4:
                    expand(s4[0], 1)
                if s2:
                    scores(*s2, 0)
                if s4:
                    expand(s4[0], 2)
                if s2:
                    queries(*s2, 1)
                    keys(*s2, 0)
                if s4:
                    contract(s4[0], 0)
                if s2:
                    scores(*s2, 1)
                if s4:
                    expand(s4[0], 3)
                if s2:
                    keys(*s2, 1)
                if s4 and not last_batch(s4[0]):
                    places(s4[0])
                if s4:
                    contract(s4[0], 1)
            steps(pe, step)

            pe.wait_ge(place_step, 4 * B)
            pe.wait_ge(place_read, B)
            nc.tensor.matmul(P_O[:, 0:E], ones_s[:], taken[:], start=True, stop=True)
            nc.tensor.matmul(P_O[:, E:2 * E], ones_s[:], taken_early[:], start=True, stop=True).then_inc(count_psum, 1)
            pe.wait_ge(table_ready, 1)

            expert = []

            def slot_step(it, turn, n):
                s1, s2, s3 = slots(it, turn, n)
                if isinstance(it, int) and it == RING - 1:
                    pe.wait_ge(table_ready, 2)
                if n % 4 == 0:
                    expert[:] = table_entries(mybir.EngineType.PE, slot_w, it, 8, (E - 1) * HC * C)
                if s1:
                    t, v, used = s1
                    pe.wait_ge(xg_loaded[v], 16 * used + 16)
                    for h in range(2):
                        for j in range(SUB):
                            last = nc.tensor.transpose(P_T[v % 2][:].bitcast(F16)[:, h * R + j * P:h * R + (j + 1) * P],
                                                       xg[v][:, j, h * C // 2:(h + 1) * C // 2].bitcast(F16), ident_h[:])
                    last.then_inc(xg_t_psum, 1)
                if s2:
                    t, v, used = s2
                    pe.wait_ge(xg_t_ready, t + 1)
                    if not s3 and positive(t - 1):
                        pe.wait_ge(hid_e_ready, t - 1)
                    pe.sem_inc(passed_pe, 1)
                    for bank, made, w in ((P_E1, e1_psum, 0), (P_E3, e3_psum, HID)):
                        for hc in range(HC):
                            at = bass.ds(expert[n % 4 + 3] * 2 + (w + hc * C), C)
                            last = split_product(bank[v % 2][:, hc * R:(hc + 1) * R], w13_h[:, at], w13_l[:, at], xg_t[v % 2])
                        last.then_inc(made, 1)
                if s3:
                    t, v, used = s3
                    pe.wait_ge(hid_e_ready, t + 1)
                    if not s2 and positive(t - 1):
                        pe.wait_ge(ye_saved, t - 1)
                    for j in range(SUB):
                        for hc in range(HC):
                            at = bass.ds(expert[n % 4 + 2] + hc * C, C)
                            last = nc.tensor.matmul(P_Y[v % 2][:, j * C:(j + 1) * C], hid_e[v % 2][:, hc, j * P:(j + 1) * P],
                                                    w2_s[:, at], start=(hc == 0), stop=(hc == HC - 1))
                    last.then_inc(ye_psum, 1)
            slot_steps(pe, slot_step)


def constants():
    n = np.arange(2 * C, dtype=np.float64) + 0.5
    cosine = np.float32(np.sqrt(4.0 / C) * np.cos(np.outer(n + C / 2, np.pi / C * n[:C]))).astype(np.float64)
    window = np.float32(np.sin(np.pi * n / (2 * C))).astype(np.float64)
    w_tok = (window[:, None] * cosine).astype(np.float32).reshape(2, C, C).transpose(1, 0, 2)
    s, t = np.arange(L)[:, None], np.arange(-1, L)[None, :]
    expo = np.maximum(s - t - 1, 0)
    bits = (expo[:, None, :] >> np.arange(BITS)[None, :, None] & 1).astype(np.float32)
    pad = np.zeros((L, TILES, TOP), np.float32)
    pad[REST:, TILES - 1, :] = 1
    pad = pad.reshape(L, TILES * TOP)
    e = np.arange(E)[None, :]
    tile = np.arange(TABLE) - LEAD
    at_end = np.arange(ENDS)[None, :]
    region_step = np.where(at_end == E, -E * CAP, CAP)
    expert_step = np.where(at_end == E, -E, 1)
    before = np.arange(L)[:, None] < np.arange(L)[None, :]
    regions = np.repeat(e * CAP, L, 0)
    return {"w_tok": w_tok, "ident": np.eye(C, dtype=np.float32)[:, None, :], "exp_bits": bits,
            "masks": np.concatenate([s > t, before], axis=1).astype(np.float32),
            "route": np.concatenate([pad * (2 * E), pad * NOWHERE, regions, np.repeat(np.arange(B)[None, :] < EARLY, L, 0)], axis=1).astype(np.float32),
            "tiles": np.concatenate([e * CAP, tile[None], R * tile[None], region_step, expert_step], axis=1).astype(np.float32)}


def kernel(x, L0_attn_basis, L0_attn_q_coeffs, L0_attn_k_coeffs, L0_attn_v_coeffs, L0_attn_o_coeffs,
           L0_attn_decay_logit, L0_attn_out_scale, L0_ffn_gate_w, L0_ffn_biases, L0_ffn_w1, L0_ffn_w3,
           L0_ffn_w2, L0_ffn_sw1, L0_ffn_sw3, L0_ffn_sw2):
    import concourse.bacc as bacc
    from concourse.bass_utils import run_bass_kernel_spmd

    f = np.float32
    padded = np.zeros((B, CHUNKS * C), f)
    padded[:, C:C + SAMPLES] = x
    t = lambda a: np.ascontiguousarray(np.asarray(a).T)
    shape_only = constants()
    across = lambda a: np.broadcast_to(np.asarray(a).reshape(1, -1), (C, np.size(a)))
    arrays = {
        "x_t": np.ascontiguousarray(padded.reshape(B, CHUNKS, C).transpose(2, 0, 1)),
        "tok_ident": np.concatenate([shape_only["w_tok"], shape_only["ident"]], axis=1),
        "coefs_t": np.stack([t(a) for a in (L0_attn_basis, L0_attn_q_coeffs, L0_attn_k_coeffs,
                                            L0_attn_v_coeffs, L0_attn_o_coeffs)], axis=1),
        "small": np.concatenate([across(L0_attn_decay_logit), across(L0_attn_out_scale), t(L0_ffn_gate_w),
                                 across(L0_ffn_biases)], axis=1),
        "exp_bits": shape_only["exp_bits"], "masks": shape_only["masks"],
        "route": shape_only["route"], "tiles": shape_only["tiles"],
        "sw13": np.concatenate([L0_ffn_sw1, L0_ffn_sw3], axis=1),
        "sw2": np.asarray(L0_ffn_sw2).reshape(HC, C, C).transpose(1, 0, 2).copy(),
        "w13": np.concatenate([L0_ffn_w1, L0_ffn_w3], axis=2).transpose(1, 0, 2).reshape(C, E * 2 * HID).copy(),
        "w2": np.asarray(L0_ffn_w2).reshape(E, HC, C, C).transpose(2, 0, 1, 3).reshape(C, E * HC * C).copy(),
    }
    names = ["x_t", "tok_ident", "coefs_t", "small", "exp_bits", "masks", "route", "tiles", "sw13", "sw2", "w13", "w2"]
    nc = bacc.Bacc("TRN2", target_bir_lowering=False, num_devices=1)
    args = [nc.dram_tensor(n, arrays[n].shape, mybir.dt.from_np(arrays[n].dtype), kind="ExternalInput").ap() for n in names]
    out = nc.dram_tensor("out", (B, FRAMES, C), F32, kind="ExternalOutput").ap()
    routed = nc.dram_tensor("routed", (ROWS, ROW), F32, kind="Internal").ap()
    results = nc.dram_tensor("results", (RESULTS, C), F32, kind="Internal").ap()
    audio_tower(nc, *args, routed, results, out)
    r = run_bass_kernel_spmd(nc, [arrays], core_ids=[0])
    return r.results[0]["out"]
```
